# Optimizing a Trainium2 kernel written in Bass

```python
import numpy as np
import jax
import jax.numpy as jnp

def _softmax(x, axis=-1):
    return jax.nn.softmax(x, axis=axis)

def _gelu(x):
    return jax.nn.gelu(x, approximate=True)

def _silu(x):
    return jax.nn.silu(x)

def _sigmoid(x):
    return jax.nn.sigmoid(x)

def _layernorm(x, axis=-1, eps=1e-05):
    m = jnp.mean(x, axis=axis, keepdims=True)
    v = jnp.var(x, axis=axis, keepdims=True)
    return (x - m) / jnp.sqrt(v + eps)

def _scatter_add(tgt, idx, src, axis=0):
    return tgt.at[idx].add(src)

def _segment_sum(src, seg, n):
    return jax.ops.segment_sum(src, seg, n)
kernel_name = 'mk_gnn_resnorm_d1_gnn_r8_b0dc7f'

def setup_inputs(seed: int=0):
    np.random.seed(seed)
    _w = jnp.asarray

    def _rec_inputs():
        import jax
        import jax.numpy as jnp
        _gk = jax.random.key(seed)
        x = -0.000202 + 1 * jax.random.normal(jax.random.fold_in(_gk, 1), (12500, 64), jnp.float32)
        src = jax.random.randint(jax.random.fold_in(_gk, 2), (200000,), 0, 12500, jnp.int32)
        dst = jax.random.randint(jax.random.fold_in(_gk, 3), (200000,), 0, 12500, jnp.int32)
        _o = jnp.argsort(dst, stable=True)
        src = src[_o]
        dst = dst[_o]
        return (x, src, dst)
    x, src, dst = _rec_inputs()

    def _L0_gnn_setup():
        import jax, jax.numpy as jnp
        import numpy as np
        N_NODES = 12500
        N_EDGES = 150000
        HID = 64
        N_LAYERS = 3
        GAMMA = -0.45
        ZETA = 1.05
        key = jax.random.key(seed)
        ks = jax.random.split(key, 8)
        s = 0.05
        return {'features': jax.random.normal(ks[0], (N_NODES, HID), jnp.float32), 'nb_W': jax.random.normal(ks[1], (N_LAYERS, HID, HID), jnp.float32) * s, 'nb_b': jnp.zeros((N_LAYERS, HID), jnp.float32), 'self_W': jax.random.normal(ks[2], (N_LAYERS, HID, HID), jnp.float32) * s, 'self_b': jnp.zeros((N_LAYERS, HID), jnp.float32), 'att1_W': jax.random.normal(ks[3], (N_LAYERS, 2 * HID, HID), jnp.float32) * s, 'att1_b': jnp.zeros((N_LAYERS, HID), jnp.float32), 'att2_W': jax.random.normal(ks[4], (N_LAYERS, HID, 1), jnp.float32) * s, 'att2_b': jnp.zeros((N_LAYERS, 1), jnp.float32), 'row': jax.random.randint(ks[5], (N_EDGES,), 0, N_NODES, jnp.int32), 'col': jax.random.randint(ks[6], (N_EDGES,), 0, N_NODES, jnp.int32)}
    _L0_gnn_all = _L0_gnn_setup()
    _L0_gnn_in = {k: v for k, v in _L0_gnn_all.items() if k in ('nb_W', 'nb_b', 'self_W', 'self_b', 'att1_W', 'att1_b', 'att2_W', 'att2_b')}
    del _L0_gnn_all
    return {'x': x, 'src': src, 'dst': dst, 'L0_gnn_nb_W': _L0_gnn_in['nb_W'], 'L0_gnn_nb_b': _L0_gnn_in['nb_b'], 'L0_gnn_self_W': _L0_gnn_in['self_W'], 'L0_gnn_self_b': _L0_gnn_in['self_b'], 'L0_gnn_att1_W': _L0_gnn_in['att1_W'], 'L0_gnn_att1_b': _L0_gnn_in['att1_b'], 'L0_gnn_att2_W': _L0_gnn_in['att2_W'], 'L0_gnn_att2_b': _L0_gnn_in['att2_b']}

def reference(x, src, dst, L0_gnn_nb_W, L0_gnn_nb_b, L0_gnn_self_W, L0_gnn_self_b, L0_gnn_att1_W, L0_gnn_att1_b, L0_gnn_att2_W, L0_gnn_att2_b):
    import jax
    import jax.numpy as jnp

    def _L0_gnn_ref(features, nb_W, nb_b, self_W, self_b, att1_W, att1_b, att2_W, att2_b, row, col):
        import jax, jax.numpy as jnp
        import numpy as np
        N_NODES = 12500
        N_EDGES = 150000
        HID = 64
        N_LAYERS = 3
        GAMMA = -0.45
        ZETA = 1.05
        n = features.shape[0]
        x = features
        out = features
        for l in range(N_LAYERS):
            f1 = jax.nn.relu(x[row] @ nb_W[l] + nb_b[l])
            f2 = jax.nn.relu(x[col] @ self_W[l] + self_b[l])
            h = jax.nn.relu(jnp.concatenate([f1, f2], axis=1) @ att1_W[l] + att1_b[l])
            log_alpha = (h @ att2_W[l] + att2_b[l])[:, 0]
            mask = jnp.clip(jax.nn.sigmoid(log_alpha) * (ZETA - GAMMA) + GAMMA, 0.0, 1.0)
            rowsum = jax.ops.segment_sum(mask, row, num_segments=n) + 1e-06
            d_inv_sqrt = jnp.clip(rowsum ** (-0.5), 0.0, 10.0)
            vals = mask * d_inv_sqrt[row] * d_inv_sqrt[col]
            x = jax.ops.segment_sum(vals[:, None] * x[col], row, num_segments=n)
            out = out + x
        return out
    x = _layernorm(x + _L0_gnn_ref(x, L0_gnn_nb_W, L0_gnn_nb_b, L0_gnn_self_W, L0_gnn_self_b, L0_gnn_att1_W, L0_gnn_att1_b, L0_gnn_att2_W, L0_gnn_att2_b, src, dst), axis=-1)
    return x

_drawn_inputs = setup_inputs


def setup_inputs(seed=0):
    import zlib

    import numpy as np

    out = dict(_drawn_inputs(seed))
    spreads = {'L0_gnn_nb_b': (0.0, 0.8),
     'L0_gnn_self_b': (0.0, 0.8),
     'L0_gnn_att1_b': (0.0, 0.8),
     'L0_gnn_att2_b': (0.0, 0.8)}
    factors = {'L0_gnn_nb_W': 8.0, 'L0_gnn_self_W': 8.0, 'L0_gnn_att1_W': 8.0, 'L0_gnn_att2_W': 8.0}
    for name, (base, spread) in spreads.items():
        noise = np.random.default_rng([zlib.crc32(name.encode()), seed]).standard_normal(out[name].shape)
        drawn = base * np.exp(spread * noise) if base else spread * noise
        out[name] = jnp.asarray(drawn.astype(out[name].dtype))
    for name, factor in factors.items():
        out[name] = (out[name] * factor).astype(out[name].dtype)
    return out
```

```python
from contextlib import ExitStack

import concourse.bass as bass
from concourse import mybir

F32 = mybir.dt.float32
BF16 = mybir.dt.bfloat16
I32 = mybir.dt.int32
ALU = mybir.AluOpType
ACT = mybir.ActivationFunctionType
AX = mybir.AxisListType
ds = bass.ds

GAMMA, ZETA = -0.45, 1.05
PARTS = 128


def ceil_div(a, b):
    return -(-a // b)


class Steps:

    def __init__(self, sem, base=0):
        self.sem, self.base, self.n = sem, base, 0

    def mark(self, instruction):
        self.n += 1
        return instruction.then_inc(self.sem, 1)

    def wait(self, engine):
        engine.wait_ge(self.sem, self.base + self.n)


def build(nc, x, src, dst, nb_W, nb_b, self_W, self_b, att1_W, att1_b, att2_W, att2_b, out):
    NODES, HID = x.shape
    EDGES = src.shape[0]
    LAYERS = nb_W.shape[0]
    U = 8
    GRP = 4
    BLOCKS = ceil_div(NODES, PARTS)
    NB = ceil_div(BLOCKS, GRP) * GRP
    FULL = NODES // PARTS
    LAST = NODES - FULL * PARTS
    EC = EDGES // PARTS
    EREST = EDGES - EC * PARTS
    SORT_STEPS = ceil_div(EC + (EREST > 0), 2 * U)
    ECP = SORT_STEPS * 2 * U
    EMPTY = ECP * PARTS - EDGES
    TILES = ceil_div(EDGES + BLOCKS * (PARTS - 1), 2 * U * PARTS) * 2 * U
    PASS_STEPS = TILES // (2 * U)
    SLOTS = max(TILES, ceil_div(EDGES + BLOCKS * (PARTS - 1) + EMPTY, PARTS))
    NONE = BLOCKS + 1
    TABLE = NB * PARTS

    ctx = ExitStack()
    with ctx:
        def sb(name, shape, dt):
            return ctx.enter_context(nc.sbuf_tensor(name, shape, dt))

        def ps(name, shape, dt):
            return ctx.enter_context(nc.psum_tensor(name, shape, dt))

        def sem(name):
            return ctx.enter_context(nc.semaphore(name))

        def two(name):
            return [sem(f"{name}{h}") for h in range(2)]

        slot_table = nc.dram_tensor("slot_table", (PARTS * SLOTS, 2), I32, kind="Internal").ap()
        q_table = nc.dram_tensor("q_table", (TABLE, HID), F32, kind="Internal").ap()
        y_table = nc.dram_tensor("y_table", (TABLE, HID), F32, kind="Internal").ap()

        iota_i = sb("iota_i", [PARTS, PARTS], I32)
        iota_b = sb("iota_b", [PARTS, PARTS], BF16)
        iota_f = sb("iota_f", [PARTS, PARTS], F32)
        part_i = sb("part_i", [PARTS, 1], I32)
        part_f = sb("part_f", [PARTS, 1], F32)
        upto = sb("upto", [PARTS, PARTS], BF16)
        after = sb("after", [PARTS, PARTS], BF16)
        before_f = sb("before_f", [PARTS, PARTS], F32)
        ident_b = sb("ident_b", [PARTS, PARTS], BF16)
        ident_f = sb("ident_f", [PARTS, PARTS], F32)
        zeros_b = sb("zeros_b", [PARTS, 512], BF16)
        ones_b = sb("ones_b", [PARTS, 1], BF16)
        real_b = sb("real_b", [PARTS, 1], BF16)
        real_t = sb("real_t", [PARTS, 1], F32)

        x_cur = sb("x_cur", [PARTS, NB, HID], F32)
        total = sb("total", [PARTS, NB, HID], F32)
        acc = sb("acc", [PARTS, NB, HID], F32)
        p3 = sb("p3", [PARTS, NB * 3 * HID], BF16)
        p3v = p3[:, :].rearrange("p (b s d) -> p b s d", s=3, d=HID)
        d_node = sb("d_node", [PARTS, NB], F32)
        rows_sum = sb("rows_sum", [PARTS, NB], F32)

        row_lo = sb("row_lo", [PARTS, TILES], F32)
        col_id = sb("col_id", [PARTS, TILES], I32)
        mask = sb("mask", [PARTS, TILES], F32)
        block_of = sb("block_of", [1, TILES], I32)

        raw = p3[:, 0:4 * ECP].bitcast(I32).rearrange("p (w c) -> p w c", w=2)
        row_in = raw[:, 0, :]
        payload = p3[:, 4 * ECP:8 * ECP].bitcast(I32).rearrange("p (c w) -> p c w", w=2)
        bucket = p3[:, 8 * ECP:10 * ECP].bitcast(F32)
        col_in = raw[:, 1, :]
        acc_flat = acc[:, :, :].rearrange("p b d -> p (b d)")
        slots_in = acc_flat[:, 0:2 * SLOTS].bitcast(I32).rearrange("p (c w) -> p c w", w=2)
        tile_i = acc_flat[:, 2 * SLOTS:2 * SLOTS + 512].bitcast(I32)
        started = acc_flat[:, 2 * SLOTS + 512:2 * SLOTS + 768].bitcast(BF16)

        w_all = sb("w_all", [HID, LAYERS, 2 * HID], F32)
        bias_all = sb("bias_all", [2 * HID, LAYERS], F32)
        a1_all = sb("a1_all", [PARTS, LAYERS, 2 * HID], F32)
        b1_all = sb("b1_all", [PARTS, LAYERS, HID], F32)
        a2_all = sb("a2_all", [PARTS, LAYERS, HID], F32)
        b2_all = sb("b2_all", [PARTS, LAYERS], F32)
        w_cur = sb("w_cur", [HID, 2 * HID], F32)
        bias_cur = sb("bias_cur", [2 * HID, 1], F32)
        a1_cur = sb("a1_cur", [PARTS, 2 * HID], F32)
        b1_cur = sb("b1_cur", [PARTS, HID], F32)
        a2_cur = sb("a2_cur", [PARTS, HID], F32)
        b2_cur = sb("b2_cur", [PARTS, 1], F32)

        onehot = [sb(f"onehot{h}", [PARTS, U, PARTS], BF16) for h in range(2)]
        onehot_t = [sb(f"onehot_t{h}", [PARTS, U, PARTS], BF16) for h in range(2)]
        weighted = [sb(f"weighted{h}", [PARTS, U, PARTS], F32) for h in range(2)]
        index = [sb(f"index{h}", [PARTS, U], I32) for h in range(2)]
        pay = [sb(f"pay{h}", [PARTS, U, 2], I32) for h in range(2)]
        got = [sb(f"got{h}", [PARTS, U, HID], F32) for h in range(2)]
        hidden = [sb(f"hidden{h}", [PARTS, U, HID], F32) for h in range(2)]
        small = [sb(f"small{h}", [PARTS, 8, U], F32) for h in range(2)]
        small_i = [sb(f"small_i{h}", [PARTS, 3, U], I32) for h in range(2)]
        mask3 = [sb(f"mask3{h}", [PARTS, U, 3], BF16) for h in range(2)]
        rank_f = [sb(f"rank_f{h}", [PARTS, U], F32) for h in range(2)]
        junk = sb("junk", [PARTS, PARTS], F32)
        row_w = [sb(f"row_w{h}", [PARTS, 2, U], F32) for h in range(2)]
        x_step = sb("x_step", [PARTS, GRP, HID], F32)
        x_t = sb("x_t", [HID, GRP * PARTS], F32)
        f_t = sb("f_t", [2 * HID, GRP * PARTS], F32)
        pq = sb("pq", [PARTS, GRP, 2 * HID], F32)
        rest = sb("rest", [PARTS, 2, GRP, HID], F32)
        q_out = sb("q_out", [PARTS, GRP, HID], F32)
        cnt = sb("cnt", [PARTS, 8], F32)
        cnt_i = sb("cnt_i", [PARTS, 2], I32)
        cnt_w = sb("cnt_w", [PARTS, PARTS], F32)
        stat = sb("stat", [PARTS, 4, NB], F32)
        eps = sb("eps", [PARTS, 1], F32)

        bank_t = [ps(f"bank_t{h}", [PARTS, U, PARTS], BF16) for h in range(2)]
        bank_p = [ps(f"bank_p{h}", [PARTS, U, HID], F32) for h in range(2)]
        bank_r = ps("bank_r", [PARTS, 512], F32)
        bank_s = ps("bank_s", [PARTS, 512], F32)
        bank_x = ps("bank_x", [PARTS, 512], F32)
        bank_m = ps("bank_m", [PARTS, 512], F32)

        s_load = sem("s_load")
        pe_go, dve_go = sem("pe_go"), sem("dve_go")
        s_iota = sem("s_iota")
        s_const = sem("s_const")
        s_fill = sem("s_fill")
        s_fillsrc = sem("s_fillsrc")
        h_onehot, h_used = two("h_onehot"), two("h_used")
        s_hist = sem("s_hist")
        s_start = sem("s_start")
        s_starts = sem("s_starts")
        s_tilei = sem("s_tilei")
        s_blk = sem("s_blk")
        s_blkuse = sem("s_blkuse")
        s_pay = two("s_pay")
        s_onehot, s_rank, s_pick, s_rest = two("s_onehot"), two("s_rank"), two("s_pick"), two("s_rest")
        s_chain = sem("s_chain")
        s_idx, s_scat, s_go = two("s_idx"), two("s_scat"), sem("s_go")
        s_back = sem("s_back")
        s_edges = sem("s_edges")
        s_zero = sem("s_zero")

        n_cur = sem("n_cur")
        n_xs = sem("n_xs")
        n_xt, n_xtc, n_f, n_fc, n_pq, n_ch, n_q = (
            sem("n_xt"), sem("n_xtc"), sem("n_f"), sem("n_fc"), sem("n_pq"), sem("n_ch"), sem("n_q"))
        n_qst = sem("n_qst")
        a_idx, a_got, a_onehot, a_tr, a_trc, a_p, a_add, a_sum, a_sig, a_m3, a_row = (
            two("a_idx"), two("a_got"), two("a_onehot"), two("a_tr"), two("a_trc"), two("a_p"),
            two("a_add"), two("a_sum"), two("a_sig"), two("a_m3"), two("a_row"))
        a_ch = sem("a_ch")
        m_zero = sem("m_zero")
        m_rows = sem("m_rows")
        m_ch, m_sqrt, m_y, m_yst, m_acc = sem("m_ch"), sem("m_sqrt"), sem("m_y"), sem("m_yst"), sem("m_acc")
        b_idx, b_row, b_got, b_w, b_o, b_acc = (
            two("b_idx"), two("b_row"), two("b_got"), two("b_w"), two("b_o"), two("b_acc"))
        b_ch = sem("b_ch")
        l_ch = sem("l_ch")
        l_end = sem("l_end")
        f_ch, f_sqrt, f_out, f_done = sem("f_ch"), sem("f_sqrt"), sem("f_out"), sem("f_done")

        LOADS = 0

        block = ctx.enter_context(nc.Block())

        @block.sync
        def _(sp):
            nonlocal LOADS

            def load(to, of):
                nonlocal LOADS
                LOADS += 16
                sp.dma_start(to, of).then_inc(s_load, 16)

            sp.wait_ge(s_zero, 1)
            for to, of in ((row_in, src), (col_in, dst)):
                load(to[:, 0:EC], of[0:EC * PARTS].rearrange("(p c) -> p c", c=EC))
                if EREST:
                    load(to[0:EREST, EC:EC + 1], of[EC * PARTS:EDGES].rearrange("(p c) -> p c", c=1))
            load(x_cur[:, 0:FULL, :], x[0:FULL * PARTS, :].rearrange("(b p) d -> p b d", p=PARTS))
            if LAST:
                load(x_cur[0:LAST, FULL, :], x[FULL * PARTS:NODES, :])
            load(w_all[:, :, 0:HID], nb_W.rearrange("l k m -> k l m"))
            load(w_all[:, :, HID:2 * HID], self_W.rearrange("l k m -> k l m"))
            load(a1_all[0:HID, :, 0:HID], att1_W[:, 0:HID, :].rearrange("l k m -> k l m"))
            load(a1_all[HID:2 * HID, :, HID:2 * HID], att1_W[:, HID:2 * HID, :].rearrange("l k m -> k l m"))
            with nc.allow_non_contiguous_dma(reason="a few hundred biases"):
                for l in range(LAYERS):
                    load(bias_all[0:HID, l:l + 1], nb_b[l].rearrange("(p c) -> p c", c=1))
                    load(bias_all[HID:2 * HID, l:l + 1], self_b[l].rearrange("(p c) -> p c", c=1))
            load(b1_all[:, :, :], att1_b.partition_broadcast(PARTS))
            load(a2_all[:, :, :], att2_W.rearrange("l k o -> l (k o)").partition_broadcast(PARTS))
            load(b2_all[:, :], att2_b.rearrange("l o -> (l o)").partition_broadcast(PARTS))
            sp.wait_ge(s_fillsrc, 1)
            sp.dma_start(slot_table.rearrange("(p c) w -> p c w", c=SLOTS), slots_in).then_inc(s_fill, 16)
            for h in range(2):
                sp.wait_ge(s_scat[h], 16 * U * SORT_STEPS)
            sp.dma_start(slots_in, slot_table.rearrange("(p c) w -> p c w", c=SLOTS)).then_inc(s_back, 16)
            with sp.Fori(0, LAYERS) as l:
                with sp.Fori(0, NB // GRP) as b:
                    sp.wait_ge(n_q, (l * (NB // GRP) + b) + 1)
                    sp.dma_start(q_table[ds(b * (GRP * PARTS), GRP * PARTS), :]
                                 .rearrange("(g p) d -> p g d", p=PARTS), q_out[:, :, :]).then_inc(n_qst, 16)
                sp.wait_ge(m_y, l + 1)
                sp.dma_start(y_table.rearrange("(b p) d -> p b d", p=PARTS), acc[:, :, :]).then_inc(m_yst, 16)
            sp.wait_ge(f_out, 1)
            sp.dma_start(out[0:FULL * PARTS, :].rearrange("(b p) d -> p b d", p=PARTS),
                         total[:, 0:FULL, :]).then_inc(f_done, 16)
            if LAST:
                sp.dma_start(out[FULL * PARTS:NODES, :], total[0:LAST, FULL, :]).then_inc(f_done, 16)
            sp.wait_ge(f_done, 16 * (1 + (LAST > 0)))

        @block.gpsimd
        def _(pool):
            pool.iota(iota_i[:, :], [[1, PARTS]], base=0, channel_multiplier=0).then_inc(s_iota, 1)
            pool.iota(part_i[:, :], [[0, 1]], base=0, channel_multiplier=1).then_inc(s_iota, 1)
            pool.wait_ge(s_fill, 16)
            with pool.Fori(0, SORT_STEPS) as g:
                for h in range(2):
                    pool.wait_ge(s_pay[h], g + 1)
                    pool.wait_ge(s_idx[h], g + 1)
                    pool.sem_inc(s_go, 1)
                    for k in range(U):
                        pool.indirect_dma_start(
                            slot_table, bass.IndirectOffsetOnAxis(ap=index[h][:, k:k + 1], axis=0),
                            pay[h][:, k, :], None).then_inc(s_scat[h], 16)
            with pool.Fori(0, LAYERS) as l:
                pool.wait_ge(n_qst, (l + 1) * (16 * (NB // GRP)))
                pool.sem_inc(s_go, 1)
                with pool.Fori(0, PASS_STEPS) as b:
                    g = l * PASS_STEPS + b
                    for h in range(2):
                        pool.wait_ge(a_idx[h], g + 1)
                        pool.wait_ge(a_add[h], g)
                        pool.sem_inc(s_go, 1)
                        for k in range(U):
                            pool.indirect_dma_start(
                                got[h][:, k, :], None, q_table,
                                bass.IndirectOffsetOnAxis(ap=index[h][:, k:k + 1], axis=0)
                            ).then_inc(a_got[h], 16)
                pool.wait_ge(m_yst, (l + 1) * 16)
                pool.sem_inc(s_go, 1)
                with pool.Fori(0, PASS_STEPS) as b:
                    g = l * PASS_STEPS + b
                    for h in range(2):
                        pool.wait_ge(b_idx[h], g + 1)
                        pool.wait_ge(b_o[h], g)
                        pool.sem_inc(s_go, 1)
                        for k in range(U):
                            pool.indirect_dma_start(
                                got[h][:, k, :], None, y_table,
                                bass.IndirectOffsetOnAxis(ap=index[h][:, k:k + 1], axis=0)
                            ).then_inc(b_got[h], 16)

        @block.tensor
        def _(pe):
            mm = nc.tensor.matmul
            pe.wait_ge(s_const, 1)
            mm(bank_m[:, 0:1], zeros_b[:, 0:PARTS], zeros_b[:, 0:1], start=True, stop=True, skip_group_check=True)
            with pe.Fori(0, SORT_STEPS) as g:
                for h in range(2):
                    pe.wait_ge(h_onehot[h], g + 1)
                    for k in range(U):
                        last = mm(bank_m[:, 0:1], onehot[h][:, k, :], ones_b[:, :], start=False, stop=True,
                                  skip_group_check=True)
                    last.then_inc(h_used[h], 1)
            mm(bank_m[:, 0:1], zeros_b[:, 0:PARTS], zeros_b[:, 0:1], start=False, stop=True,
               skip_group_check=True).then_inc(s_hist, 1)
            pe.wait_ge(s_start, 1)
            mm(bank_x[:, 0:1], before_f[:, :], cnt[:, 1:2], start=True, stop=True).then_inc(s_starts, 1)
            mm(bank_s[:, 0:PARTS], cnt_w[:, :], before_f[:, :], start=True, stop=True, skip_group_check=True)
            for c, at in enumerate(range(0, TILES, 512)):
                w = min(512, TILES - at)
                pe.wait_ge(s_blk, c + 1)
                mm(bank_m[0:1, 0:w], real_b[:, :], started[:, 0:w], start=True, stop=True,
                   skip_group_check=True).then_inc(s_blkuse, 1)
            with pe.Fori(0, SORT_STEPS) as g:
                for h in range(2):
                    pe.wait_ge(s_onehot[h], g + 1)
                    for k in range(U):
                        mm(bank_s[:, 0:PARTS], upto[:, :], onehot[h][:, k, :], start=False, stop=True,
                           skip_group_check=True).then_inc(s_rank[h], 1)
                        pe.wait_ge(s_pick[h], g * U + (k + 1))
                        mm(bank_s[:, 0:PARTS], after[:, :], onehot[h][:, k, :], start=False, stop=True,
                           skip_group_check=True).then_inc(s_rest[h], 1)
            blk = [pe.alloc_register(f"pe_blk{k}") for k in range(U)]
            pe.wait_ge(s_edges, 1)

            def blocks(at):
                pe.load(blk, block_of[0:1, ds(at, U)])
                return [pe.snap(r, min_val=0, max_val=BLOCKS - 1) for r in blk]

            with pe.Fori(0, LAYERS) as l:
                pe.wait_ge(n_cur, l + 1)
                pe.sem_inc(pe_go, 1)
                with pe.Fori(0, NB // GRP) as b:
                    n = l * (NB // GRP) + b
                    pe.wait_ge(n_xs, n + 1)
                    pe.wait_ge(n_xtc, n)
                    pe.sem_inc(pe_go, 1)
                    for j in range(GRP):
                        last = nc.tensor.transpose(bank_x[0:HID, j * PARTS:(j + 1) * PARTS],
                                                   x_step[:, j, :], ident_f[:, :])
                    last.then_inc(n_xt, 1)
                    pe.wait_ge(n_xtc, n + 1)
                    mm(bank_m[:, :], w_cur[:, :], x_t[:, :], start=True, stop=True).then_inc(n_f, 1)
                    pe.wait_ge(n_fc, n + 1)
                    pe.wait_ge(n_q, n)
                    for j in range(GRP):
                        last = mm(bank_s[:, j * PARTS:(j + 1) * PARTS], f_t[:, j * PARTS:(j + 1) * PARTS],
                                  a1_cur[:, :], start=True, stop=True)
                    last.then_inc(n_pq, 1)
                mm(bank_r[:, :], zeros_b[:, 0:PARTS], zeros_b[:, :], start=True, stop=True, skip_group_check=True)
                with pe.Fori(0, PASS_STEPS) as b:
                    g = l * PASS_STEPS + b
                    for h in range(2):
                        at = blocks((b * 2 + h) * U)
                        pe.wait_ge(a_onehot[h], g + 1)
                        pe.wait_ge(a_trc[h], g)
                        for k in range(U):
                            last = nc.tensor.transpose(bank_t[h][:, k, :], onehot[h][:, k, :], ident_b[:, :])
                        last.then_inc(a_tr[h], 1)
                        pe.wait_ge(a_trc[h], g + 1)
                        pe.wait_ge(a_add[h], g)
                        for k in range(U):
                            for s in range(3):
                                last = mm(bank_p[h][:, k, :], onehot_t[h][:, k, :],
                                          p3v[:, ds(at[k], 1), s, :].rearrange("p o d -> p (o d)"),
                                          start=(s == 0), stop=(s == 2))
                        last.then_inc(a_p[h], 1)
                        pe.wait_ge(a_m3[h], g + 1)
                        for k in range(U):
                            last = mm(bank_r[:, ds(at[k] * 4, 3)], onehot[h][:, k, :], mask3[h][:, k, :],
                                      start=False, stop=True, skip_group_check=True)
                        last.then_inc(a_row[h], 1)
                mm(bank_r[:, 0:4], zeros_b[:, 0:PARTS], zeros_b[:, 0:4], start=False, stop=True,
                   skip_group_check=True).then_inc(m_rows, 1)
                with pe.Fori(0, PASS_STEPS) as b:
                    g = l * PASS_STEPS + b
                    for h in range(2):
                        pe.wait_ge(b_w[h], g + 1)
                        pe.wait_ge(b_got[h], (g + 1) * (16 * U))
                        pe.wait_ge(b_acc[h], g)
                        for k in range(U):
                            last = mm(bank_p[h][:, k, :], weighted[h][:, k, :], got[h][:, k, :],
                                      start=True, stop=True)
                        last.then_inc(b_o[h], 1)

        @block.scalar
        def _(act):
            a = nc.scalar
            act.wait_ge(s_const, 2)
            with act.Fori(0, SORT_STEPS) as g:
                for h in range(2):
                    act.wait_ge(s_scat[h], g * (16 * U))
                    a.copy(pay[h][:, :, :], payload[:, ds((g * 2 + h) * U, U), :]).then_inc(s_pay[h], 1)
            act.wait_ge(s_edges, 1)
            with act.Fori(0, LAYERS) as l:
                act.wait_ge(n_cur, l + 1)
                with act.Fori(0, NB // GRP) as b:
                    n = l * (NB // GRP) + b
                    act.wait_ge(n_xt, n)
                    a.copy(x_step[:, :, :], x_cur[:, ds(b * GRP, GRP), :]).then_inc(n_xs, 1)
                    act.wait_ge(n_xt, n + 1)
                    act.wait_ge(n_f, n)
                    a.copy(x_t[:, :], bank_x[0:HID, :]).then_inc(n_xtc, 1)
                    act.wait_ge(n_f, n + 1)
                    act.wait_ge(n_pq, n)
                    a.activation(f_t[:, :], bank_m[:, :], ACT.Relu, bias=bias_cur[:, :]).then_inc(n_fc, 1)
                with act.Fori(0, PASS_STEPS) as b:
                    g = l * PASS_STEPS + b
                    for h in range(2):
                        act.wait_ge(a_got[h], g * (16 * U))
                        a.copy(index[h][:, :], col_id[:, ds((b * 2 + h) * U, U)]).then_inc(a_idx[h], 1)
                        act.wait_ge(a_tr[h], g + 1)
                        act.wait_ge(a_p[h], g)
                        a.copy(onehot_t[h][:, :, :], bank_t[h][:, :, :]).then_inc(a_trc[h], 1)
                        act.wait_ge(a_sum[h], g + 1)
                        a.activation(small[h][:, 1, :], small[h][:, 0, :], ACT.Sigmoid,
                                     bias=b2_cur[:, :]).then_inc(a_sig[h], 1)
                act.wait_ge(m_ch, l * 4 + 3)
                a.activation(stat[:, 0, :], rows_sum[:, :], ACT.Sqrt).then_inc(m_sqrt, 1)
                with act.Fori(0, PASS_STEPS) as b:
                    g = l * PASS_STEPS + b
                    for h in range(2):
                        at = (b * 2 + h) * U
                        act.wait_ge(b_got[h], g * (16 * U))
                        a.copy(index[h][:, :], col_id[:, ds(at, U)]).then_inc(b_idx[h], 1)
                        act.wait_ge(b_w[h], g)
                        a.copy(row_w[h][:, 0, :], row_lo[:, ds(at, U)])
                        a.copy(row_w[h][:, 1, :], mask[:, ds(at, U)]).then_inc(b_row[h], 1)
            act.wait_ge(f_ch, 8)
            a.activation(stat[:, 2, :], stat[:, 1, :], ACT.Sqrt, bias=eps[:, :], scale=1.0 / HID).then_inc(f_sqrt, 1)

        @block.vector
        def _(dve):
            v = nc.vector
            c = Steps(s_chain)

            def link(instruction):
                c.mark(instruction)
                c.wait(dve)

            v.memset(row_in[:, EC:ECP], NONE * PARTS)
            v.memset(col_in[:, EC:ECP], 0)
            v.memset(x_cur[:, FULL:NB, :], 0.0)
            v.memset(slots_in[:, :, 0], PARTS)
            v.memset(slots_in[:, :, 1], 0)
            link(v.memset(a1_all[:, :, :], 0.0))
            v.memset(zeros_b[:, :], 0.0).then_inc(s_zero, 1)
            v.memset(ones_b[:, :], 1.0).then_inc(s_fillsrc, 1)
            v.memset(eps[:, :], 1e-5)
            dve.wait_ge(s_iota, 2)
            v.tensor_copy(iota_b[:, :], iota_i[:, :])
            v.tensor_copy(iota_f[:, :], iota_i[:, :])
            link(v.tensor_copy(part_f[:, :], part_i[:, :]))
            v.tensor_scalar(upto[:, :], iota_f[:, :], part_f[:, :], None, ALU.is_ge)
            v.tensor_scalar(after[:, :], iota_f[:, :], part_f[:, :], None, ALU.is_lt)
            v.tensor_scalar(before_f[:, :], iota_f[:, :], part_f[:, :], None, ALU.is_gt)
            v.tensor_scalar(ident_b[:, :], iota_f[:, :], part_f[:, :], None, ALU.is_equal)
            v.tensor_scalar(ident_f[:, :], iota_f[:, :], part_f[:, :], None, ALU.is_equal)
            link(v.tensor_scalar(real_t[:, :], part_f[:, :], 0.5, None, ALU.is_gt))
            v.scalar_tensor_tensor(out=real_b[:, :], in0=part_f[:, :], scalar=float(BLOCKS) - 0.5,
                                   in1=real_t[:, :], op0=ALU.is_lt, op1=ALU.mult).then_inc(s_const, 1)
            dve.wait_ge(s_load, LOADS)
            shift = PARTS.bit_length() - 1
            v.tensor_scalar(payload[:, :, 0], row_in, PARTS - 1, None, ALU.bitwise_and)
            v.tensor_copy(payload[:, :, 1], col_in)
            link(v.tensor_scalar(row_in, row_in, shift, None, ALU.logical_shift_right))
            c.mark(v.tensor_copy(bucket, row_in))
            c.wait(dve)
            v.tensor_scalar(col_in, row_in, NONE, None, ALU.is_equal).then_inc(s_zero, 1)
            dve.wait_ge(s_zero, 2)
            c.mark(v.scalar_tensor_tensor(out=payload[:, :, 0], in0=col_in, scalar=float(PARTS),
                                          in1=payload[:, :, 0], op0=ALU.mult, op1=ALU.add))
            c.wait(dve)
            v.tensor_copy(junk[:, 0:1], part_f[:, :]).then_inc(s_const, 1)

            def build_onehot(to, of):
                n = of.shape[1]
                return v.tensor_tensor(to, iota_b[:, :].unsqueeze(1).to_broadcast([PARTS, n, PARTS]),
                                       of.unsqueeze(2).to_broadcast([PARTS, n, PARTS]), ALU.is_equal)

            with dve.Fori(0, SORT_STEPS) as g:
                for h in range(2):
                    dve.wait_ge(h_used[h], g)
                    build_onehot(onehot[h][:, :, :], bucket[:, ds((g * 2 + h) * U, U)]).then_inc(h_onehot[h], 1)
            dve.wait_ge(s_hist, 1)
            link(v.tensor_scalar(cnt_i[:, 0:1], bank_m[:, 0:1], float(PARTS - 1), None, ALU.add))
            link(v.tensor_scalar(cnt_i[:, 1:2], cnt_i[:, 0:1], shift, None, ALU.logical_shift_right))
            link(v.tensor_copy(cnt[:, 1:2], cnt_i[:, 1:2]))
            link(v.tensor_scalar(cnt[:, 2:3], cnt[:, 1:2], float(PARTS), None, ALU.mult))
            v.tensor_copy(cnt_w[:, :], cnt[:, 2:3].to_broadcast([PARTS, PARTS])).then_inc(s_start, 1)
            dve.wait_ge(s_starts, 1)
            link(v.tensor_copy(cnt[:, 3:4], bank_x[:, 0:1]))
            for n, at in enumerate(range(0, TILES, 512)):
                w = min(512, TILES - at)
                for q in range(0, w, PARTS):
                    m = min(PARTS, w - q)
                    link(v.tensor_scalar(junk[:, 0:m], iota_f[:, 0:m], float(at + q), None, ALU.add))
                    c.mark(v.tensor_scalar(started[:, q:q + m], junk[:, 0:m], cnt[:, 3:4], None, ALU.is_ge))
                    c.wait(dve)
                v.tensor_copy(junk[:, 0:1], part_f[:, :]).then_inc(s_blk, 1)
                dve.wait_ge(s_blkuse, n + 1)
                link(v.tensor_copy(block_of[0:1, at:at + w], bank_m[0:1, 0:w]))
            with dve.Fori(0, SORT_STEPS) as g:
                for h in range(2):
                    dve.wait_ge(s_rest[h], g * U)
                    build_onehot(onehot[h][:, :, :], bucket[:, ds((g * 2 + h) * U, U)]).then_inc(s_onehot[h], 1)
                    dve.wait_ge(s_onehot[h], g + 1)
                    for k in range(U):
                        dve.wait_ge(s_rank[h], g * U + (k + 1))
                        v.tensor_tensor_reduce(out=junk[:, :], in0=bank_s[:, 0:PARTS], in1=onehot[h][:, k, :],
                                               scale=1.0, scalar=0.0, op0=ALU.mult, op1=ALU.add,
                                               accum_out=rank_f[h][:, k:k + 1]).then_inc(s_pick[h], 1)
                    dve.wait_ge(s_pick[h], (g + 1) * U)
                    e = Steps(b_ch, (g * 2 + h) * 3)
                    i = small_i[h]
                    e.mark(v.tensor_scalar(i[:, 0, :], rank_f[h][:, :], -1.0, None, ALU.add))
                    e.wait(dve)
                    v.tensor_scalar(i[:, 1, :], i[:, 0, :], PARTS - 1, None, ALU.bitwise_and)
                    e.mark(v.tensor_scalar(i[:, 2, :], i[:, 0, :], shift, None, ALU.logical_shift_right))
                    e.wait(dve)
                    dve.wait_ge(s_scat[h], g * (16 * U))
                    v.scalar_tensor_tensor(out=index[h][:, :], in0=i[:, 1, :], scalar=float(SLOTS),
                                           in1=i[:, 2, :], op0=ALU.mult, op1=ALU.add).then_inc(s_idx[h], 1)
                    e.mark(v.memset(junk[:, 0:1], 0.0))
            SORTED = SORT_STEPS * 6
            dve.wait_ge(s_back, 16)
            v.tensor_copy(row_lo[:, :], slots_in[:, 0:TILES, 0])
            c.mark(v.tensor_copy(col_id[:, :], slots_in[:, 0:TILES, 1]))
            v.tensor_scalar(total[:, :, :], x_cur[:, :, :], 2.0, None, ALU.mult)
            c.wait(dve)
            v.memset(junk[:, 0:1], 0.0).then_inc(s_edges, 1)

            blk = [dve.alloc_register(f"dve_blk{k}") for k in range(U)]
            NODE_STEPS = NB // GRP
            with dve.Fori(0, LAYERS) as l:
                for cur, every in ((w_cur, w_all), (a1_cur, a1_all), (b1_cur, b1_all), (a2_cur, a2_all)):
                    v.tensor_copy(cur[:, :], every[:, ds(l, 1), :].rearrange("p o d -> p (o d)"))
                v.tensor_copy(bias_cur[:, :], bias_all[:, ds(l, 1)])
                v.tensor_copy(b2_cur[:, :], b2_all[:, ds(l, 1)]).then_inc(n_cur, 1)
                dve.wait_ge(n_cur, l + 1)
                dve.sem_inc(dve_go, 1)
                with dve.Fori(0, NODE_STEPS) as b:
                    n = l * NODE_STEPS + b
                    e = Steps(n_ch, n * 6)
                    part = p3v[:, ds(b * GRP, GRP), :, :]
                    dve.wait_ge(n_pq, n + 1)
                    both = bank_s[:, :].rearrange("p (g d) -> p g d", g=GRP)
                    e.mark(v.tensor_tensor(rest[:, 0, :, :], both[:, :, 0:HID],
                                           b1_cur[:, :].unsqueeze(1).to_broadcast([PARTS, GRP, HID]), ALU.add))
                    dve.wait_ge(n_qst, n * 16)
                    v.tensor_copy(q_out[:, :, :], both[:, :, HID:2 * HID]).then_inc(n_q, 1)
                    e.wait(dve)
                    e.mark(v.tensor_copy(part[:, :, 0, :], rest[:, 0, :, :]))
                    e.wait(dve)
                    e.mark(v.tensor_tensor(rest[:, 1, :, :], rest[:, 0, :, :], part[:, :, 0, :], ALU.subtract))
                    e.wait(dve)
                    e.mark(v.tensor_copy(part[:, :, 1, :], rest[:, 1, :, :]))
                    e.wait(dve)
                    e.mark(v.tensor_tensor(part[:, :, 2, :], rest[:, 1, :, :], part[:, :, 1, :], ALU.subtract))
                    e.mark(v.memset(junk[:, 0:1], 0.0))
                    e.wait(dve)
                with dve.Fori(0, PASS_STEPS) as b:
                    g = l * PASS_STEPS + b
                    for h in range(2):
                        at = (b * 2 + h) * U
                        e = Steps(a_ch, (g * 2 + h) * 7)
                        sm = small[h]
                        dve.wait_ge(a_row[h], g)
                        build_onehot(onehot[h][:, :, :], row_lo[:, ds(at, U)]).then_inc(a_onehot[h], 1)
                        dve.wait_ge(a_p[h], g + 1)
                        dve.wait_ge(a_got[h], (g + 1) * (16 * U))
                        v.tensor_tensor(hidden[h][:, :, :], bank_p[h][:, :, :], got[h][:, :, :],
                                        ALU.add).then_inc(a_add[h], 1)
                        dve.wait_ge(a_add[h], g + 1)
                        e.mark(v.scalar_tensor_tensor(out=hidden[h][:, :, :], in0=hidden[h][:, :, :], scalar=0.0,
                                                      in1=a2_cur[:, :].unsqueeze(1).to_broadcast([PARTS, U, HID]),
                                                      op0=ALU.max, op1=ALU.mult))
                        e.wait(dve)
                        v.tensor_reduce(sm[:, 0, :], hidden[h][:, :, :], AX.X, ALU.add).then_inc(a_sum[h], 1)
                        dve.wait_ge(a_sig[h], g + 1)
                        e.mark(v.tensor_scalar(sm[:, 2, :], sm[:, 1, :], ZETA - GAMMA, GAMMA, ALU.mult, ALU.add))
                        e.wait(dve)
                        e.mark(v.tensor_scalar(sm[:, 3, :], sm[:, 2, :], 0.0, 1.0, ALU.max, ALU.min))
                        e.wait(dve)
                        m3 = mask3[h]
                        v.tensor_copy(mask[:, ds(at, U)], sm[:, 3, :])
                        e.mark(v.tensor_copy(m3[:, :, 0], sm[:, 3, :]))
                        e.wait(dve)
                        e.mark(v.tensor_tensor(sm[:, 4, :], sm[:, 3, :], m3[:, :, 0], ALU.subtract))
                        e.wait(dve)
                        e.mark(v.tensor_copy(m3[:, :, 1], sm[:, 4, :]))
                        e.wait(dve)
                        v.tensor_tensor(m3[:, :, 2], sm[:, 4, :], m3[:, :, 1], ALU.subtract).then_inc(a_m3[h], 1)
                        e.mark(v.memset(junk[:, 0:1], 0.0))
                e = Steps(m_ch, l * 4)
                dve.wait_ge(m_rows, l + 1)
                sums = bank_r[:, 0:4 * NB].rearrange("p (b s) -> p b s", s=4)
                e.mark(v.tensor_reduce(rows_sum[:, :], sums[:, :, 0:3], AX.X, ALU.add))
                e.wait(dve)
                e.mark(v.tensor_scalar(rows_sum[:, :], rows_sum[:, :], 1e-6, None, ALU.add))
                e.wait(dve)
                e.mark(v.memset(junk[:, 0:1], 0.0))
                dve.wait_ge(m_sqrt, l + 1)
                e.mark(v.reciprocal(stat[:, 1, :], stat[:, 0, :]))
                e.wait(dve)
                v.tensor_scalar(d_node[:, :], stat[:, 1, :], 10.0, None, ALU.min).then_inc(m_acc, 1)
                dve.wait_ge(m_acc, l * 2 + 1)
                d_wide = d_node[:, :].unsqueeze(2).to_broadcast([PARTS, NB, HID])
                v.tensor_tensor(acc[:, :, :], x_cur[:, :, :], d_wide, ALU.mult).then_inc(m_y, 1)
                dve.wait_ge(m_yst, (l + 1) * 16)
                v.memset(acc[:, :, :], 0.0).then_inc(m_acc, 1)
                dve.wait_ge(m_acc, l * 2 + 2)
                dve.sem_inc(dve_go, 1)
                with dve.Fori(0, PASS_STEPS) as b:
                    g = l * PASS_STEPS + b
                    for h in range(2):
                        dve.load(blk, block_of[0:1, ds((b * 2 + h) * U, U)])
                        at = [dve.snap(r, min_val=0, max_val=BLOCKS - 1) for r in blk]
                        dve.wait_ge(b_row[h], g + 1)
                        dve.wait_ge(b_o[h], g)
                        for k in range(U):
                            last = v.tensor_scalar(weighted[h][:, k, :], iota_f[:, :], row_w[h][:, 0, k:k + 1],
                                                   row_w[h][:, 1, k:k + 1], ALU.is_equal, ALU.mult)
                        last.then_inc(b_w[h], 1)
                        dve.wait_ge(b_o[h], g + 1)
                        for k in range(U):
                            one = acc[:, ds(at[k], 1), :].rearrange("p o d -> p (o d)")
                            last = v.tensor_tensor(one, one, bank_p[h][:, k, :], ALU.add)
                            last.then_inc(b_acc[h] if k == U - 1 else l_ch, 1)
                            if k < U - 1:
                                dve.wait_ge(l_ch, (g * 2 + h) * (U - 1) + (k + 1))
                        dve.wait_ge(b_acc[h], g + 1)
                v.tensor_tensor(x_cur[:, :, :], acc[:, :, :], d_wide, ALU.mult).then_inc(l_end, 1)
                dve.wait_ge(l_end, l * 2 + 1)
                v.tensor_tensor(total[:, :, :], total[:, :, :], x_cur[:, :, :], ALU.add).then_inc(l_end, 1)
                dve.wait_ge(l_end, l * 2 + 2)
            e = Steps(f_ch)

            def chained(instruction):
                e.mark(instruction)
                e.wait(dve)

            wide = [PARTS, NB, HID]
            chained(v.tensor_reduce(stat[:, 0, :], total[:, :, :], AX.X, ALU.add))
            chained(v.tensor_scalar(stat[:, 3, :], stat[:, 0, :], 1.0 / HID, None, ALU.mult))
            chained(v.tensor_tensor(total[:, :, :], total[:, :, :], stat[:, 3, :].unsqueeze(2).to_broadcast(wide),
                                    ALU.subtract))
            chained(v.tensor_tensor(acc[:, :, :], total[:, :, :], total[:, :, :], ALU.mult))
            chained(v.tensor_reduce(stat[:, 1, :], acc[:, :, :], AX.X, ALU.add))
            chained(v.memset(junk[:, 0:1], 0.0))
            chained(v.memset(junk[:, 0:1], 0.0))
            chained(v.memset(junk[:, 0:1], 0.0))
            dve.wait_ge(f_sqrt, 1)
            chained(v.reciprocal(stat[:, 0, :], stat[:, 2, :]))
            v.tensor_tensor(total[:, :, :], total[:, :, :], stat[:, 0, :].unsqueeze(2).to_broadcast(wide),
                            ALU.mult).then_inc(f_out, 1)


NAMES = {"x": "x", "src": "src", "dst": "dst", "L0_gnn_nb_W": "nb_W", "L0_gnn_nb_b": "nb_b",
         "L0_gnn_self_W": "self_W", "L0_gnn_self_b": "self_b", "L0_gnn_att1_W": "att1_W",
         "L0_gnn_att1_b": "att1_b", "L0_gnn_att2_W": "att2_W", "L0_gnn_att2_b": "att2_b"}


def kernel(**inputs):
    import numpy as np
    import concourse.bacc as bacc
    from concourse.bass_utils import run_bass_kernel_spmd

    nc = bacc.Bacc("TRN2", target_bir_lowering=False, num_devices=1)
    arrays, args = {}, {}
    for name, arg in NAMES.items():
        a = np.ascontiguousarray(inputs[name])
        arrays[f"in_{arg}"] = a
        args[arg] = nc.dram_tensor(f"in_{arg}", a.shape, mybir.dt.from_np(a.dtype), kind="ExternalInput").ap()
    shape = inputs["x"].shape
    args["out"] = nc.dram_tensor("out_0", shape, F32, kind="ExternalOutput").ap()
    build(nc, **args)
    r = run_bass_kernel_spmd(nc, [arrays], core_ids=[0])
    return r.results[0]["out_0"]
```

```python
from contextlib import ExitStack

import concourse.bass as bass
from concourse import mybir

F32 = mybir.dt.float32
BF16 = mybir.dt.bfloat16
I32 = mybir.dt.int32
ALU = mybir.AluOpType
ACT = mybir.ActivationFunctionType
AX = mybir.AxisListType
ds = bass.ds

GAMMA, ZETA = -0.45, 1.05
PARTS = 128


def ceil_div(a, b):
    return -(-a // b)


class Steps:

    def __init__(self, sem, base=0):
        self.sem, self.base, self.n = sem, base, 0

    def mark(self, instruction):
        self.n += 1
        return instruction.then_inc(self.sem, 1)

    def wait(self, engine):
        engine.wait_ge(self.sem, self.base + self.n)


def build(nc, x, src, dst, nb_W, nb_b, self_W, self_b, att1_W, att1_b, att2_W, att2_b, out):
    NODES, HID = x.shape
    EDGES = src.shape[0]
    LAYERS = nb_W.shape[0]
    U = 8
    GRP = 4
    BLOCKS = ceil_div(NODES, PARTS)
    NODE_STEPS = ceil_div(BLOCKS, 2 * GRP)
    NB = NODE_STEPS * 2 * GRP
    FULL = NODES // PARTS
    LAST = NODES - FULL * PARTS
    EC = EDGES // PARTS
    EREST = EDGES - EC * PARTS
    SORT_STEPS = ceil_div(EC + (EREST > 0), 2 * U)
    ECP = SORT_STEPS * 2 * U
    EMPTY = ECP * PARTS - EDGES
    TILES = ceil_div(EDGES + BLOCKS * PARTS, 4 * U * PARTS) * 4 * U
    A_STEPS = TILES // (2 * U)
    B_STEPS = TILES // (4 * U)
    AHEAD = 4 * U
    SLOTS = max(TILES, ceil_div(EDGES + (BLOCKS + 1) * PARTS + EMPTY, PARTS))
    NONE = BLOCKS + 1
    TABLE = NB * PARTS

    ctx = ExitStack()
    with ctx:
        def sb(name, shape, dt):
            return ctx.enter_context(nc.sbuf_tensor(name, shape, dt))

        def sem(name):
            return ctx.enter_context(nc.semaphore(name))

        def two(name):
            return [sem(f"{name}{h}") for h in range(2)]

        slot_table = nc.dram_tensor("slot_table", (PARTS * SLOTS, 2), I32, kind="Internal").ap()
        qx_table = nc.dram_tensor("qx_table", (TABLE, 2 * HID), F32, kind="Internal").ap()
        y_table = nc.dram_tensor("y_table", (TABLE, HID), F32, kind="Internal").ap()
        kept_x = nc.dram_tensor("kept_x", (A_STEPS * PARTS, U * HID), F32, kind="Internal").ap()

        iota_i = sb("iota_i", [PARTS, PARTS], I32)
        iota_b = sb("iota_b", [PARTS, PARTS], BF16)
        iota_f = sb("iota_f", [PARTS, PARTS], F32)
        part_i = sb("part_i", [PARTS, 1], I32)
        part_f = sb("part_f", [PARTS, 1], F32)
        upto = sb("upto", [PARTS, PARTS], BF16)
        after = sb("after", [PARTS, PARTS], BF16)
        before_f = sb("before_f", [PARTS, PARTS], F32)
        ident_b = sb("ident_b", [PARTS, PARTS], BF16)
        ident_f = sb("ident_f", [PARTS, PARTS], F32)
        zeros_b = sb("zeros_b", [PARTS, 512], BF16)
        ones_f = sb("ones_f", [PARTS, 1], F32)
        real_b = sb("real_b", [PARTS, 1], BF16)
        real_t = sb("real_t", [PARTS, 1], F32)
        eps = sb("eps", [PARTS, 1], F32)

        x_cur = sb("x_cur", [PARTS, NB, HID], F32)
        total = sb("total", [PARTS, NB, HID], F32)
        acc = sb("acc", [PARTS, NB + U, HID], F32)
        p3 = sb("p3", [PARTS, NB * 3 * HID], BF16)
        p3v = p3[:, :].rearrange("p (b s d) -> p b s d", s=3, d=HID)
        d_node = sb("d_node", [PARTS, NB], F32)
        d3 = sb("d3", [PARTS, 3, NB], BF16)
        rows_sum = sb("rows_sum", [PARTS, NB], F32)
        stat = sb("stat", [PARTS, 4, NB], F32)

        row_lo = sb("row_lo", [PARTS, TILES + AHEAD], BF16)
        col_lo = sb("col_lo", [PARTS, TILES + AHEAD], BF16)
        col_hi = sb("col_hi", [PARTS, TILES + AHEAD], BF16)
        col_id = sb("col_id", [PARTS, TILES + AHEAD], I32)
        mask = sb("mask", [PARTS, TILES + AHEAD], F32)
        block_of = sb("block_of", [1, TILES + AHEAD], mybir.dt.int16)
        spot_of = sb("spot_of", [1, TILES], mybir.dt.int16)

        raw = p3[:, 0:4 * ECP].bitcast(I32).rearrange("p (w c) -> p w c", w=2)
        row_in = raw[:, 0, :]
        col_in = raw[:, 1, :]
        payload = p3[:, 4 * ECP:8 * ECP].bitcast(I32).rearrange("p (c w) -> p c w", w=2)
        bucket = p3[:, 8 * ECP:9 * ECP]
        acc_flat = acc[:, :, :].rearrange("p b d -> p (b d)")
        slots_in = acc_flat[:, 0:2 * SLOTS].bitcast(I32).rearrange("p (c w) -> p c w", w=2)
        started = acc_flat[:, 2 * SLOTS:2 * SLOTS + 256].bitcast(BF16)
        counts = acc_flat[:, 2 * SLOTS + 256:2 * SLOTS + 256 + PARTS]
        lane_hits = acc_flat[:, 2 * SLOTS + 384:2 * SLOTS + 384 + ECP // 2].bitcast(BF16)
        col_tmp = x_cur[:, :, :].rearrange("p b d -> p (b d)")[:, 0:TILES].bitcast(I32)

        w_all = sb("w_all", [HID, LAYERS, 2 * HID], F32)
        bias_all = sb("bias_all", [2 * HID, LAYERS], F32)
        a1_all = sb("a1_all", [PARTS, LAYERS, 2 * HID], F32)
        b1_all = sb("b1_all", [PARTS, LAYERS, HID], F32)
        a2_all = sb("a2_all", [PARTS, LAYERS, HID], F32)
        b2_all = sb("b2_all", [PARTS, LAYERS], F32)
        w_cur = sb("w_cur", [HID, 2 * HID], F32)
        bias_cur = sb("bias_cur", [2 * HID, 1], F32)
        a1_cur = sb("a1_cur", [PARTS, 2 * HID], F32)
        b1_cur = sb("b1_cur", [PARTS, HID], F32)
        a2_cur = sb("a2_cur", [PARTS, HID], F32)
        b2_cur = sb("b2_cur", [PARTS, 1], F32)

        def ring(name, shape, dt):
            return [sb(f"{name}{h}", shape, dt) for h in range(2)]

        onehot = ring("onehot", [PARTS, U, PARTS], BF16)
        onehot_t = ring("onehot_t", [PARTS, U, PARTS], BF16)
        index = ring("index", [PARTS, U], I32)
        pay = ring("pay", [PARTS, U, 2], I32)
        got = ring("got", [PARTS, U, 2 * HID], F32)
        hidden = ring("hidden", [PARTS, U, HID], F32)
        small = ring("small", [PARTS, 8, U], F32)
        small_i = ring("small_i", [PARTS, 3, U], I32)
        mask3 = ring("mask3", [PARTS, U, 3], BF16)
        rank_f = ring("rank_f", [PARTS, U], F32)
        junk = sb("junk", [PARTS, PARTS], F32)
        g_mask = ring("g_mask", [PARTS, U], F32)
        g_hot = sb("g_hot", [PARTS, U, PARTS], F32)
        k_edge = ring("k_edge", [PARTS, 2, U], F32)
        k_d = ring("k_d", [PARTS, 2, U], F32)
        k_hot = sb("k_hot", [PARTS, U, PARTS], F32)
        k_x = ring("k_x", [PARTS, U, HID], F32)
        x_t = [g_hot[0:HID, h * GRP:(h + 1) * GRP, :].rearrange("p g m -> p (g m)") for h in range(2)]
        f_t = [k_hot[:, h * GRP:(h + 1) * GRP, :].rearrange("p g m -> p (g m)") for h in range(2)]
        qx = ring("qx", [PARTS, GRP, 2 * HID], F32)
        rest = [hidden[h][:, :, :].rearrange("p (w g) d -> p w g d", w=2) for h in range(2)]
        cnt = sb("cnt", [PARTS, 4], F32)
        cnt_i = sb("cnt_i", [PARTS, 2], I32)
        cnt_w = sb("cnt_w", [PARTS, PARTS], F32)

        bank = [ctx.enter_context(nc.psum_tensor(f"bank{i}", [PARTS, 512], F32)) for i in range(8)]
        bank_t = [bank[h][:, :].bitcast(BF16).rearrange("p (k m) -> p k m", k=U) for h in range(2)]
        bank_p = [bank[2 + h][:, :].rearrange("p (k d) -> p k d", k=U) for h in range(2)]
        bank_r = bank[6]
        bank_s = bank[4]
        bank_d = [[bank[4 + 2 * j + q][:, :].rearrange("p (k m) -> p k m", k=U // 2) for q in range(2)]
                  for j in range(2)]

        s_rows, s_load = sem("s_rows"), sem("s_load")
        pool_go, pe_go, dve_go, sp_go = sem("pool_go"), sem("pe_go"), sem("dve_go"), sem("sp_go")
        s_iota, s_const, s_open, s_fillsrc, s_fill = (
            sem("s_iota"), sem("s_const"), sem("s_open"), sem("s_fillsrc"), sem("s_fill"))
        s_edges_in = sem("s_edges_in")
        s_chain, s_count = sem("s_chain"), sem("s_count")
        s_hist, s_tiles, s_starts, s_blk, s_blkuse = (
            sem("s_hist"), sem("s_tiles"), sem("s_starts"), sem("s_blk"), sem("s_blkuse"))
        s_pay, s_onehot, s_rank, s_pick, s_rest, s_idx, s_scat = (
            two("s_pay"), two("s_onehot"), two("s_rank"), two("s_pick"), two("s_rest"), two("s_idx"), two("s_scat"))
        s_slot = sem("s_slot")
        s_back, s_edges = sem("s_back"), sem("s_edges")
        n_cur = sem("n_cur")
        n_x, n_xt, n_xtc, n_f, n_fc, n_pq, n_q, n_qst = (
            two("n_x"), two("n_xt"), two("n_xtc"), two("n_f"), two("n_fc"), two("n_pq"), two("n_q"), two("n_qst"))
        n_ch = sem("n_ch")
        a_idx, a_got, a_kept, a_onehot, a_tr, a_trc, a_p, a_add, a_sum, a_sig, a_m3, a_row = (
            two("a_idx"), two("a_got"), sem("a_kept"), two("a_onehot"), two("a_tr"), two("a_trc"), two("a_p"),
            two("a_add"), two("a_sum"), two("a_sig"), two("a_m3"), two("a_row"))
        a_ch = sem("a_ch")
        k_xs, g_xs, k_wd = sem("k_xs"), sem("g_xs"), sem("k_wd")
        m_rows, m_ch, m_sqrt, m_d, m_y, m_yst = (
            sem("m_rows"), sem("m_ch"), sem("m_sqrt"), sem("m_d"), sem("m_y"), sem("m_yst"))
        g_idx, g_edges, g_got, g_w, g_o, g_acc = (
            two("g_idx"), two("g_edges"), two("g_got"), sem("g_w"), two("g_o"), sem("g_acc"))
        k_edges, k_xin, k_onehot, k_tr, k_trc, k_w, k_o, k_acc = (
            two("k_edges"), two("k_xin"), two("k_onehot"), two("k_tr"), two("k_trc"), sem("k_w"), two("k_o"),
            sem("k_acc"))
        k_rows = [two("k_rows_a"), two("k_rows_b")]
        k_sel = [two("k_sel_a"), two("k_sel_b")]
        l_end = sem("l_end")
        f_ch, f_sqrt, f_out, f_done = sem("f_ch"), sem("f_sqrt"), sem("f_out"), sem("f_done")

        ROW_LOADS = 16 * (1 + (EREST > 0))
        loads = [0]
        GOT = 16 * U
        block = ctx.enter_context(nc.Block())

        @block.sync
        def _(sp):
            def load(to, of):
                loads[0] += 16
                sp.dma_start(to, of).then_inc(s_load, 16)

            sp.wait_ge(s_open, 1)
            for to, of, signal in ((row_in, src, s_rows), (col_in, dst, s_load)):
                sp.dma_start(to[:, 0:EC], of[0:EC * PARTS].rearrange("(p c) -> p c", c=EC)).then_inc(signal, 16)
                if EREST:
                    sp.dma_start(to[0:EREST, EC:EC + 1],
                                 of[EC * PARTS:EDGES].rearrange("(p c) -> p c", c=1)).then_inc(signal, 16)
            loads[0] += ROW_LOADS
            sp.wait_ge(s_fillsrc, 1)
            sp.dma_start(slot_table.rearrange("(p c) w -> p c w", c=SLOTS), slots_in).then_inc(s_fill, 16)
            load(total[:, 0:FULL, :], x[0:FULL * PARTS, :].rearrange("(b p) d -> p b d", p=PARTS))
            if LAST:
                load(total[0:LAST, FULL, :], x[FULL * PARTS:NODES, :])
            load(w_all[:, :, 0:HID], nb_W.rearrange("l k m -> k l m"))
            load(w_all[:, :, HID:2 * HID], self_W.rearrange("l k m -> k l m"))
            load(a1_all[0:HID, :, 0:HID], att1_W[:, 0:HID, :].rearrange("l k m -> k l m"))
            load(a1_all[HID:2 * HID, :, HID:2 * HID], att1_W[:, HID:2 * HID, :].rearrange("l k m -> k l m"))
            with nc.allow_non_contiguous_dma(reason="a few hundred biases"):
                for l in range(LAYERS):
                    load(bias_all[0:HID, l:l + 1], nb_b[l].rearrange("(p c) -> p c", c=1))
                    load(bias_all[HID:2 * HID, l:l + 1], self_b[l].rearrange("(p c) -> p c", c=1))
            load(b1_all[:, :, :], att1_b.partition_broadcast(PARTS))
            load(a2_all[:, :, :], att2_W.rearrange("l k o -> l (k o)").partition_broadcast(PARTS))
            load(b2_all[:, :], att2_b.rearrange("l o -> (l o)").partition_broadcast(PARTS))
            for h in range(2):
                sp.wait_ge(s_scat[h], GOT * SORT_STEPS)
            sp.dma_start(slots_in, slot_table.rearrange("(p c) w -> p c w", c=SLOTS)).then_inc(s_back, 16)
            with sp.Fori(0, LAYERS) as l:
                with sp.Fori(0, NODE_STEPS) as b:
                    for h in range(2):
                        sp.wait_ge(n_q[h], l * NODE_STEPS + b + 1)
                        sp.dma_start(qx_table[ds((b * 2 + h) * (GRP * PARTS), GRP * PARTS), :]
                                     .rearrange("(g p) d -> p g d", p=PARTS), qx[h][:, :, :]).then_inc(n_qst[h], 16)
                with sp.Fori(0, A_STEPS) as b:
                    sp.wait_ge(a_got[1], (l * A_STEPS + b + 1) * GOT)
                    sp.dma_start(kept_x[ds(b * PARTS, PARTS), :].rearrange("p (k d) -> p k d", k=U),
                                 got[1][:, :, HID:2 * HID]).then_inc(a_kept, 16)
                sp.wait_ge(m_y, l + 1)
                sp.dma_start(y_table.rearrange("(b p) d -> p b d", p=PARTS), x_cur[:, :, :]).then_inc(m_yst, 16)
                sp.wait_ge(a_kept, (l + 1) * (16 * A_STEPS))
                sp.sem_inc(sp_go, 1)
                with sp.Fori(0, B_STEPS) as b:
                    for j in range(2):
                        sp.wait_ge(k_o[j], l * B_STEPS + b)
                        sp.dma_start(k_x[j][:, :, :], kept_x[ds((b * 2 + j) * PARTS, PARTS), :]
                                     .rearrange("p (k d) -> p k d", k=U)).then_inc(k_xin[j], 16)
            sp.wait_ge(f_out, 1)
            sp.dma_start(out[0:FULL * PARTS, :].rearrange("(b p) d -> p b d", p=PARTS),
                         total[:, 0:FULL, :]).then_inc(f_done, 16)
            if LAST:
                sp.dma_start(out[FULL * PARTS:NODES, :], total[0:LAST, FULL, :]).then_inc(f_done, 16)
            sp.wait_ge(f_done, 16 * (1 + (LAST > 0)))

        @block.gpsimd
        def _(pool):
            pool.iota(iota_i[:, :], [[1, PARTS]], base=0, channel_multiplier=0).then_inc(s_iota, 1)
            pool.iota(part_i[:, :], [[0, 1]], base=0, channel_multiplier=1).then_inc(s_iota, 1)
            pool.wait_ge(s_fill, 16)
            with pool.Fori(0, SORT_STEPS) as g:
                for h in range(2):
                    pool.wait_ge(s_pay[h], g + 1)
                    pool.wait_ge(s_idx[h], g + 1)
                    pool.sem_inc(pool_go, 1)
                    for k in range(U):
                        pool.indirect_dma_start(
                            slot_table, bass.IndirectOffsetOnAxis(ap=index[h][:, k:k + 1], axis=0),
                            pay[h][:, k, :], None).then_inc(s_scat[h], 16)
            with pool.Fori(0, LAYERS) as l:
                pool.wait_ge(n_cur, l + 1)
                pool.sem_inc(pool_go, 1)
                with pool.Fori(0, NODE_STEPS) as b:
                    n = l * NODE_STEPS + b
                    for h in range(2):
                        pool.wait_ge(n_qst[h], n * 16)
                        pool.sem_inc(pool_go, 1)
                        pool.tensor_copy(qx[h][:, :, HID:2 * HID],
                                         x_cur[:, ds((b * 2 + h) * GRP, GRP), :]).then_inc(n_x[h], 1)
                for h in range(2):
                    pool.wait_ge(n_qst[h], (l + 1) * (16 * NODE_STEPS))
                pool.sem_inc(pool_go, 1)
                with pool.Fori(0, A_STEPS) as b:
                    g = l * A_STEPS + b
                    for h in range(2):
                        pool.wait_ge(a_idx[h], l * (A_STEPS + 1) + b + 1)
                        pool.wait_ge(a_add[h], g)
                        if h == 1:
                            pool.wait_ge(a_kept, g * 16)
                        pool.sem_inc(pool_go, 1)
                        for k in range(U):
                            pool.indirect_dma_start(
                                got[h][:, k, :], None, qx_table,
                                bass.IndirectOffsetOnAxis(ap=index[h][:, k:k + 1], axis=0)
                            ).then_inc(a_got[h], 16)
                pool.wait_ge(a_kept, (l + 1) * (16 * A_STEPS))
                pool.wait_ge(m_yst, (l + 1) * 16)
                pool.sem_inc(pool_go, 1)
                with pool.Fori(0, B_STEPS) as b:
                    for j in range(2):
                        pool.wait_ge(g_idx[j], l * (B_STEPS + 1) + b + 1)
                        pool.wait_ge(g_o[j], l * B_STEPS + b)
                        pool.sem_inc(pool_go, 1)
                        for k in range(U):
                            pool.indirect_dma_start(
                                got[j][:, k, 0:HID], None, y_table,
                                bass.IndirectOffsetOnAxis(ap=index[j][:, k:k + 1], axis=0)
                            ).then_inc(g_got[j], 16)

        @block.tensor
        def _(pe):
            mm = nc.tensor.matmul
            turn = nc.tensor.transpose

            def plus(to, lhsT, rhs):
                return mm(to, lhsT, rhs, start=False, stop=True, skip_group_check=True)

            pe.wait_ge(s_const, 1)
            pe.wait_ge(s_count, BLOCKS)
            mm(bank[5][:, 0:1], counts, ones_f[:, :], start=True, stop=True).then_inc(s_hist, 1)
            pe.wait_ge(s_tiles, 1)
            mm(bank[7][:, 0:1], before_f[:, :], cnt[:, 1:2], start=True, stop=True).then_inc(s_starts, 1)
            mm(bank_s[:, 0:PARTS], cnt_w[:, :], before_f[:, :], start=True, stop=True, skip_group_check=True)
            with pe.Fori(0, SORT_STEPS) as g:
                for h in range(2):
                    pe.wait_ge(s_onehot[h], g + 1)
                    for k in range(U):
                        plus(bank_s[:, 0:PARTS], upto[:, :], onehot[h][:, k, :]).then_inc(s_rank[h], 1)
                        pe.wait_ge(s_pick[h], g * U + (k + 1))
                        plus(bank_s[:, 0:PARTS], after[:, :], onehot[h][:, k, :]).then_inc(s_rest[h], 1)
            for c, at in enumerate(range(0, TILES, 512)):
                w = min(512, TILES - at)
                pe.wait_ge(s_blk, c + 1)
                mm(bank[5][0:1, 0:w], real_b[:, :], started[:, 0:w], start=True, stop=True).then_inc(s_blkuse, 1)
            pe.wait_ge(s_edges, 1)
            blk = [pe.alloc_register(f"pe_blk{k}") for k in range(U)]

            with pe.Fori(0, LAYERS) as l:
                pe.wait_ge(n_cur, l + 1)
                pe.sem_inc(pe_go, 1)
                with pe.Fori(0, NODE_STEPS) as b:
                    n = l * NODE_STEPS + b
                    for h in range(2):
                        pe.wait_ge(n_x[h], n + 1)
                        pe.sem_inc(pe_go, 1)
                        for i in range(GRP):
                            last = turn(bank[h][0:HID, i * PARTS:(i + 1) * PARTS], qx[h][:, i, HID:2 * HID],
                                        ident_f[:, :])
                        last.then_inc(n_xt[h], 1)
                    for h in range(2):
                        pe.wait_ge(n_xtc[h], n + 1)
                        mm(bank[2 + h][:, :], w_cur[:, :], x_t[h], start=True, stop=True).then_inc(n_f[h], 1)
                    for h in range(2):
                        pe.wait_ge(n_fc[h], n + 1)
                        pe.wait_ge(n_q[h], n)
                        for i in range(GRP):
                            last = mm(bank[4 + h][:, i * PARTS:(i + 1) * PARTS], f_t[h][:, i * PARTS:(i + 1) * PARTS],
                                      a1_cur[:, :], start=True, stop=True)
                        last.then_inc(n_pq[h], 1)
                mm(bank_r[:, :], zeros_b[:, 0:PARTS], zeros_b[:, :], start=True, stop=True, skip_group_check=True)

                def spread(h, at, used, read):
                    pe.load(blk, block_of[0:1, ds(at, U)])
                    ids = [pe.snap(r, min_val=0, max_val=BLOCKS - 1) for r in blk]
                    pe.wait_ge(a_onehot[h], used + 1)
                    for k in range(U):
                        last = turn(bank_t[h][:, k, :], onehot[h][:, k, :], ident_b[:, :])
                    last.then_inc(a_tr[h], 1)
                    pe.wait_ge(a_trc[h], used + 1)
                    pe.wait_ge(a_add[h], read)
                    for k in range(U):
                        for s in range(3):
                            last = mm(bank_p[h][:, k, :], onehot_t[h][:, k, :],
                                      p3v[:, ds(ids[k], 1), s, :].rearrange("p o d -> p (o d)"),
                                      start=(s == 0), stop=(s == 2))
                    last.then_inc(a_p[h], 1)

                spread(0, 0, l * (A_STEPS + 1), l * A_STEPS)
                with pe.Fori(0, A_STEPS) as b:
                    g = l * A_STEPS + b
                    for h in range(2):
                        spread(1 - h, (b * 2 + (h + 1)) * U, [g, l * (A_STEPS + 1) + b + 1][h], g + h)
                        pe.load(blk, block_of[0:1, ds((b * 2 + h) * U, U)])
                        at = [pe.snap(r, min_val=0, max_val=BLOCKS - 1) for r in blk]
                        pe.wait_ge(a_m3[h], g + 1)
                        for k in range(U):
                            last = plus(bank_r[:, ds(at[k] * 4, 3)], onehot[h][:, k, :], mask3[h][:, k, :])
                        last.then_inc(a_row[h], 1)
                plus(bank_r[:, 0:4], zeros_b[:, 0:PARTS], zeros_b[:, 0:4]).then_inc(m_rows, 1)

                def turn_columns(j, n):
                    pe.wait_ge(k_onehot[j], n)
                    for k in range(U):
                        last = turn(bank_t[j][:, k, :], onehot[j][:, k, :], ident_b[:, :])
                    last.then_inc(k_tr[j], 1)

                turn_columns(0, l * (B_STEPS + 1) + 1)
                with pe.Fori(0, B_STEPS) as b:
                    g = l * B_STEPS + b
                    for j in range(2):
                        used = [l * (B_STEPS + 1) + b, g]
                        pe.wait_ge(k_trc[j], used[j] + 1)
                        for q in range(2):
                            pe.wait_ge(k_sel[j][q], g)
                            for k in range(U // 2):
                                for s in range(3):
                                    last = mm(bank_d[j][q][:, k, 0:NB], onehot_t[j][:, q * (U // 2) + k, :],
                                              d3[:, s, :], start=(s == 0), stop=(s == 2))
                            last.then_inc(k_rows[j][q], 1)
                        turn_columns(1 - j, [g, l * (B_STEPS + 1) + b + 1][j] + 1)
                        n = g * 2 + (j + 1)
                        for bank_o, hot, rows, hot_ready, rows_ready, read, done, at in (
                                (bank[2], k_hot, k_x[j], k_w, k_xs, k_acc, k_o[j], (b * 4 + (2 * j + 1)) * U),
                                (bank[3], g_hot, got[j], g_w, g_xs, g_acc, g_o[j], (b * 4 + 2 * j) * U)):
                            pe.load(blk, spot_of[0:1, ds(at, U)])
                            spot = [pe.snap(r, min_val=0, max_val=(U - 1) * HID) for r in blk]
                            pe.wait_ge(read, n - 1)
                            mm(bank_o[:, :], zeros_b[:, 0:PARTS], zeros_b[:, :], start=True, stop=True,
                               skip_group_check=True)
                            pe.wait_ge(hot_ready, n)
                            pe.wait_ge(rows_ready, n)
                            for k in range(U):
                                last = plus(bank_o[:, ds(spot[k], HID)], hot[:, k, :], rows[:, k, 0:HID])
                            last.then_inc(done, 1)
                pe.wait_ge(k_trc[0], (l + 1) * (B_STEPS + 1))
                pe.sem_inc(pe_go, 1)

        @block.scalar
        def _(act):
            a = nc.scalar
            act.wait_ge(s_edges_in, 1)
            with act.Fori(0, SORT_STEPS) as g:
                for h in range(2):
                    act.wait_ge(s_scat[h], g * GOT)
                    a.copy(pay[h][:, :, :], payload[:, ds((g * 2 + h) * U, U), :]).then_inc(s_pay[h], 1)
            act.wait_ge(s_edges, 1)
            with act.Fori(0, LAYERS) as l:
                with act.Fori(0, NODE_STEPS) as b:
                    n = l * NODE_STEPS + b
                    for h in range(2):
                        act.wait_ge(n_xt[h], n + 1)
                        a.copy(x_t[h], bank[h][0:HID, :]).then_inc(n_xtc[h], 1)
                    for h in range(2):
                        act.wait_ge(n_f[h], n + 1)
                        act.wait_ge(n_pq[h], n)
                        a.activation(f_t[h], bank[2 + h][:, :], ACT.Relu, bias=bias_cur[:, :]).then_inc(n_fc[h], 1)
                for h in range(2):
                    act.wait_ge(g_idx[h], l * (B_STEPS + 1))
                    a.copy(index[h][:, :], col_id[:, h * U:(h + 1) * U]).then_inc(a_idx[h], 1)

                def spread_turned(h, used):
                    act.wait_ge(a_tr[h], used + 1)
                    act.wait_ge(a_p[h], used)
                    a.copy(onehot_t[h][:, :, :], bank_t[h]).then_inc(a_trc[h], 1)

                spread_turned(0, l * (A_STEPS + 1))
                with act.Fori(0, A_STEPS) as b:
                    g = l * A_STEPS + b
                    for h in range(2):
                        spread_turned(1 - h, [g, l * (A_STEPS + 1) + b + 1][h])
                        act.wait_ge(a_sum[h], g + 1)
                        a.activation(small[h][:, 1, :], small[h][:, 7, :], ACT.Exp, scale=-1.0).then_inc(a_sig[h], 1)
                        act.wait_ge(a_got[h], (g + 1) * GOT)
                        a.copy(index[h][:, :], col_id[:, ds((b * 2 + 2 + h) * U, U)]).then_inc(a_idx[h], 1)
                act.wait_ge(m_ch, l * 8 + 2)
                a.activation(stat[:, 0, :], rows_sum[:, :], ACT.Sqrt).then_inc(m_sqrt, 1)

                def gather_edges(j, at):
                    a.copy(index[j][:, :], col_id[:, ds(at, U)]).then_inc(g_idx[j], 1)
                    a.copy(g_mask[j][:, :], mask[:, ds(at, U)]).then_inc(g_edges[j], 1)

                def look_edges(j, at):
                    a.copy(k_edge[j][:, 0, :], mask[:, ds(at, U)])
                    a.copy(k_edge[j][:, 1, :], col_hi[:, ds(at, U)]).then_inc(k_edges[j], 1)

                def turned(j, n, g):
                    act.wait_ge(k_tr[j], n)
                    act.wait_ge(k_rows[j][1], g)
                    a.copy(onehot_t[j][:, :, :], bank_t[j]).then_inc(k_trc[j], 1)

                for j in range(2):
                    act.wait_ge(a_idx[j], (l + 1) * (A_STEPS + 1))
                    act.wait_ge(g_edges[j], l * (B_STEPS + 1))
                    act.wait_ge(k_edges[j], l * (B_STEPS + 1))
                    gather_edges(j, 2 * j * U)
                    look_edges(j, (2 * j + 1) * U)
                turned(0, l * (B_STEPS + 1) + 1, l * B_STEPS)
                with act.Fori(0, B_STEPS) as b:
                    g = l * B_STEPS + b
                    for j in range(2):
                        turned(1 - j, [g, l * (B_STEPS + 1) + b + 1][j] + 1, g + j)
                        act.wait_ge(k_xin[j], (g + 1) * 16)
                        act.wait_ge(k_wd, g * 2 + (j + 1))
                        for k in range(U):
                            last = a.activation(k_x[j][:, k, :], k_x[j][:, k, :], ACT.Copy, scale=k_d[j][:, 1, k:k + 1])
                        last.then_inc(k_xs, 1)
                        look_edges(j, (b * 4 + (2 * j + 5)) * U)
                        act.wait_ge(g_got[j], (g + 1) * GOT)
                        act.wait_ge(g_edges[j], l * (B_STEPS + 1) + b + 1)
                        for k in range(U):
                            last = a.activation(got[j][:, k, 0:HID], got[j][:, k, 0:HID], ACT.Copy,
                                                scale=g_mask[j][:, k:k + 1])
                        last.then_inc(g_xs, 1)
                        act.wait_ge(g_xs, g * 2 + (j + 1))
                        gather_edges(j, (b * 4 + (2 * j + 4)) * U)
            act.wait_ge(f_ch, 5)
            a.activation(stat[:, 2, :], stat[:, 1, :], ACT.Sqrt, bias=eps[:, :], scale=1.0 / HID).then_inc(f_sqrt, 1)

        @block.vector
        def _(dve):
            v = nc.vector
            c = Steps(s_chain)
            shift = PARTS.bit_length() - 1

            def link(instruction, steps=None):
                (steps or c).mark(instruction)
                (steps or c).wait(dve)

            v.memset(row_in[:, EC:ECP], NONE * PARTS)
            v.memset(col_in[:, EC:ECP], 0)
            v.memset(total[:, FULL:NB, :], 0.0)
            v.memset(a1_all[:, :, :], 0.0).then_inc(s_open, 1)
            v.memset(slots_in[:, :, 0], PARTS)
            v.memset(slots_in[:, :, 1], 0).then_inc(s_fillsrc, 1)
            v.memset(zeros_b[:, :], 0.0)
            v.memset(ones_f[:, :], 1.0)
            v.memset(eps[:, :], 1e-5)
            v.memset(counts, 0.0)
            for edges in (row_lo, col_lo, col_hi, col_id, mask):
                v.memset(edges[:, TILES:TILES + AHEAD], 0)
            dve.wait_ge(s_iota, 2)
            v.tensor_copy(iota_b[:, :], iota_i[:, :])
            v.tensor_copy(iota_f[:, :], iota_i[:, :])
            link(v.tensor_copy(part_f[:, :], part_i[:, :]))
            v.tensor_scalar(upto[:, :], iota_f[:, :], part_f[:, :], None, ALU.is_ge)
            v.tensor_scalar(after[:, :], iota_f[:, :], part_f[:, :], None, ALU.is_lt)
            v.tensor_scalar(before_f[:, :], iota_f[:, :], part_f[:, :], None, ALU.is_gt)
            v.tensor_scalar(ident_b[:, :], iota_f[:, :], part_f[:, :], None, ALU.is_equal)
            v.tensor_scalar(ident_f[:, :], iota_f[:, :], part_f[:, :], None, ALU.is_equal)
            link(v.tensor_scalar(real_t[:, :], part_f[:, :], 0.5, None, ALU.is_gt))
            v.scalar_tensor_tensor(out=real_b[:, :], in0=part_f[:, :], scalar=float(BLOCKS) - 0.5,
                                   in1=real_t[:, :], op0=ALU.is_lt, op1=ALU.mult).then_inc(s_const, 1)
            dve.wait_ge(s_rows, ROW_LOADS)
            v.tensor_scalar(payload[:, :, 0], row_in, PARTS - 1, None, ALU.bitwise_and)
            link(v.tensor_scalar(row_in, row_in, shift, None, ALU.logical_shift_right))
            link(v.tensor_copy(bucket, row_in))
            with dve.Fori(0, BLOCKS) as b:
                v.tensor_scalar(lane_hits, bucket, iota_f[:, ds(b, 1)], 0.0, ALU.is_equal, ALU.add,
                                accum_out=counts[:, ds(b, 1)]).then_inc(s_count, 1)
                dve.wait_ge(s_count, b + 1)
            dve.wait_ge(s_load, loads[0])
            v.tensor_copy(payload[:, :, 1], col_in)
            link(v.tensor_scalar(row_in, row_in, NONE, None, ALU.is_equal))
            v.scalar_tensor_tensor(out=payload[:, :, 0], in0=row_in, scalar=float(PARTS), in1=payload[:, :, 0],
                                   op0=ALU.mult, op1=ALU.add).then_inc(s_edges_in, 1)
            dve.wait_ge(s_hist, 1)
            link(v.tensor_scalar(cnt_i[:, 0:1], bank[5][:, 0:1], float(PARTS - 1), None, ALU.add))
            link(v.tensor_scalar(cnt_i[:, 1:2], cnt_i[:, 0:1], shift, None, ALU.logical_shift_right))
            link(v.tensor_scalar(cnt[:, 1:2], cnt_i[:, 1:2], 1.0, None, ALU.max))
            link(v.tensor_scalar(cnt[:, 2:3], cnt[:, 1:2], float(PARTS), None, ALU.mult))
            v.tensor_copy(cnt_w[:, :], cnt[:, 2:3].to_broadcast([PARTS, PARTS])).then_inc(s_tiles, 1)

            def build_onehot(to, of):
                wide = [PARTS, U, PARTS]
                return v.tensor_tensor(to[:, :, :], iota_b[:, :].unsqueeze(1).to_broadcast(wide),
                                       of.unsqueeze(2).to_broadcast(wide), ALU.is_equal)

            with dve.Fori(0, SORT_STEPS) as g:
                for h in range(2):
                    dve.wait_ge(s_rest[h], g * U)
                    build_onehot(onehot[h], bucket[:, ds((g * 2 + h) * U, U)]).then_inc(s_onehot[h], 1)
                    dve.wait_ge(s_onehot[h], g + 1)
                    for k in range(U):
                        dve.wait_ge(s_rank[h], g * U + (k + 1))
                        v.tensor_tensor_reduce(out=junk[:, :], in0=bank_s[:, 0:PARTS], in1=onehot[h][:, k, :],
                                               scale=1.0, scalar=0.0, op0=ALU.mult, op1=ALU.add,
                                               accum_out=rank_f[h][:, k:k + 1]).then_inc(s_pick[h], 1)
                    dve.wait_ge(s_pick[h], (g + 1) * U)
                    e = Steps(s_slot, (g * 2 + h) * 2)
                    i = small_i[h]
                    link(v.tensor_scalar(i[:, 0, :], rank_f[h][:, :], -1.0, None, ALU.add), e)
                    v.tensor_scalar(i[:, 1, :], i[:, 0, :], PARTS - 1, None, ALU.bitwise_and)
                    link(v.tensor_scalar(i[:, 2, :], i[:, 0, :], shift, None, ALU.logical_shift_right), e)
                    dve.wait_ge(s_scat[h], g * GOT)
                    v.scalar_tensor_tensor(out=index[h][:, :], in0=i[:, 1, :], scalar=float(SLOTS),
                                           in1=i[:, 2, :], op0=ALU.mult, op1=ALU.add).then_inc(s_idx[h], 1)
            dve.wait_ge(s_starts, 1)
            link(v.tensor_copy(cnt[:, 3:4], bank[7][:, 0:1]))
            for n, at in enumerate(range(0, TILES, 512)):
                w = min(512, TILES - at)
                for q in range(0, w, PARTS):
                    m = min(PARTS, w - q)
                    last = v.tensor_scalar(started[:, q:q + m], iota_f[:, 0:m], float(at + q), cnt[:, 3:4],
                                           ALU.add, ALU.is_ge)
                last.then_inc(s_blk, 1)
                dve.wait_ge(s_blkuse, n + 1)
                link(v.tensor_copy(block_of[0:1, at:at + w], bank[5][0:1, 0:w]))
            v.memset(block_of[0:1, TILES:TILES + AHEAD], BLOCKS - 1)
            steps_wide = [1, TILES // U, U]
            by_step = block_of[0:1, 0:TILES].rearrange("p (t k) -> p t k", k=U)
            spots = spot_of[0:1, :].rearrange("p (t k) -> p t k", k=U)
            link(v.tensor_tensor(spots, by_step, by_step[:, :, 0:1].to_broadcast(steps_wide), ALU.subtract))
            link(v.tensor_scalar(spot_of[0:1, :], spot_of[0:1, :], float(HID), None, ALU.mult))
            link(v.tensor_scalar(total[:, :, :], total[:, :, :], 2.0, None, ALU.mult))
            dve.wait_ge(s_back, 16)
            slot_col = slots_in[:, 0:TILES, 1]
            v.tensor_copy(row_lo[:, 0:TILES], slots_in[:, 0:TILES, 0])
            v.tensor_copy(col_id[:, 0:TILES], slot_col)
            link(v.tensor_scalar(col_tmp, slot_col, shift, None, ALU.logical_shift_right))
            link(v.tensor_copy(col_hi[:, 0:TILES], col_tmp))
            link(v.tensor_scalar(col_tmp, slot_col, PARTS - 1, None, ALU.bitwise_and))
            link(v.tensor_copy(col_lo[:, 0:TILES], col_tmp))
            v.tensor_scalar(x_cur[:, :, :], total[:, :, :], 0.5, None, ALU.mult).then_inc(s_edges, 1)
            dve.wait_ge(s_edges, 1)

            blk = dve.alloc_register("dve_blk")
            with dve.Fori(0, LAYERS) as l:
                for cur, every in ((w_cur, w_all), (a1_cur, a1_all), (b1_cur, b1_all), (a2_cur, a2_all)):
                    v.tensor_copy(cur[:, :], every[:, ds(l, 1), :].rearrange("p o d -> p (o d)"))
                v.tensor_copy(bias_cur[:, :], bias_all[:, ds(l, 1)])
                v.tensor_copy(b2_cur[:, :], b2_all[:, ds(l, 1)]).then_inc(n_cur, 1)
                dve.wait_ge(n_cur, l + 1)
                dve.sem_inc(dve_go, 1)
                with dve.Fori(0, NODE_STEPS) as b:
                    n = l * NODE_STEPS + b
                    for h in range(2):
                        e = Steps(n_ch, (n * 2 + h) * 5)
                        part = p3v[:, ds((b * 2 + h) * GRP, GRP), :, :]
                        both = bank[4 + h][:, :].rearrange("p (g d) -> p g d", g=GRP)
                        dve.wait_ge(n_pq[h], n + 1)
                        e.mark(v.tensor_tensor(rest[h][:, 0], both[:, :, 0:HID],
                                               b1_cur[:, :].unsqueeze(1).to_broadcast([PARTS, GRP, HID]), ALU.add))
                        dve.wait_ge(n_qst[h], n * 16)
                        v.tensor_copy(qx[h][:, :, 0:HID], both[:, :, HID:2 * HID]).then_inc(n_q[h], 1)
                        e.wait(dve)
                        link(v.tensor_copy(part[:, :, 0, :], rest[h][:, 0]), e)
                        link(v.tensor_tensor(rest[h][:, 1], rest[h][:, 0], part[:, :, 0, :],
                                             ALU.subtract), e)
                        link(v.tensor_copy(part[:, :, 1, :], rest[h][:, 1]), e)
                        e.mark(v.tensor_tensor(part[:, :, 2, :], rest[h][:, 1], part[:, :, 1, :], ALU.subtract))
                def spread_onehot(h, at, freed):
                    dve.wait_ge(a_row[h], freed)
                    build_onehot(onehot[h], row_lo[:, ds(at, U)]).then_inc(a_onehot[h], 1)

                spread_onehot(0, 0, l * A_STEPS)
                with dve.Fori(0, A_STEPS) as b:
                    g = l * A_STEPS + b
                    for h in range(2):
                        at = (b * 2 + h) * U
                        e = Steps(a_ch, (g * 2 + h) * 9)
                        sm, m3 = small[h], mask3[h]
                        spread_onehot(1 - h, (b * 2 + (h + 1)) * U, g + h)
                        dve.wait_ge(a_p[h], [l * (A_STEPS + 1) + b, g][h] + 1)
                        dve.wait_ge(a_got[h], (g + 1) * GOT)
                        v.tensor_tensor(hidden[h][:, :, :], bank_p[h], got[h][:, :, 0:HID], ALU.add).then_inc(a_add[h], 1)
                        dve.wait_ge(a_add[h], g + 1)
                        link(v.scalar_tensor_tensor(out=hidden[h][:, :, :], in0=hidden[h][:, :, :], scalar=0.0,
                                                    in1=a2_cur[:, :].unsqueeze(1).to_broadcast([PARTS, U, HID]),
                                                    op0=ALU.max, op1=ALU.mult), e)
                        link(v.tensor_reduce(sm[:, 0, :], hidden[h][:, :, :], AX.X, ALU.add), e)
                        v.tensor_scalar(sm[:, 7, :], sm[:, 0, :], b2_cur[:, :], -80.0, ALU.add,
                                        ALU.max).then_inc(a_sum[h], 1)
                        dve.wait_ge(a_sig[h], g + 1)
                        link(v.tensor_scalar(sm[:, 5, :], sm[:, 1, :], 1.0, None, ALU.add), e)
                        link(v.reciprocal(sm[:, 6, :], sm[:, 5, :]), e)
                        link(v.tensor_scalar(sm[:, 2, :], sm[:, 6, :], ZETA - GAMMA, GAMMA, ALU.mult, ALU.add), e)
                        link(v.tensor_scalar(sm[:, 3, :], sm[:, 2, :], 0.0, 1.0, ALU.max, ALU.min), e)
                        v.tensor_copy(mask[:, ds(at, U)], sm[:, 3, :])
                        link(v.tensor_copy(m3[:, :, 0], sm[:, 3, :]), e)
                        link(v.tensor_tensor(sm[:, 4, :], sm[:, 3, :], m3[:, :, 0], ALU.subtract), e)
                        link(v.tensor_copy(m3[:, :, 1], sm[:, 4, :]), e)
                        v.tensor_tensor(m3[:, :, 2], sm[:, 4, :], m3[:, :, 1], ALU.subtract).then_inc(a_m3[h], 1)
                e = Steps(m_ch, l * 8)
                dve.wait_ge(m_rows, l + 1)
                sums = bank_r[:, 0:4 * NB].rearrange("p (b s) -> p b s", s=4)
                link(v.tensor_reduce(rows_sum[:, :], sums[:, :, 0:3], AX.X, ALU.add), e)
                e.mark(v.tensor_scalar(rows_sum[:, :], rows_sum[:, :], 1e-6, None, ALU.add))
                dve.wait_ge(m_sqrt, l + 1)
                link(v.reciprocal(stat[:, 1, :], stat[:, 0, :]), e)
                link(v.tensor_scalar(d_node[:, :], stat[:, 1, :], 10.0, None, ALU.min), e)
                d_wide = d_node[:, :].unsqueeze(2).to_broadcast([PARTS, NB, HID])
                v.tensor_tensor(x_cur[:, :, :], x_cur[:, :, :], d_wide, ALU.mult).then_inc(m_y, 1)
                link(v.tensor_copy(d3[:, 0, :], d_node[:, :]), e)
                link(v.tensor_tensor(stat[:, 2, :], d_node[:, :], d3[:, 0, :], ALU.subtract), e)
                link(v.tensor_copy(d3[:, 1, :], stat[:, 2, :]), e)
                v.tensor_tensor(d3[:, 2, :], stat[:, 2, :], d3[:, 1, :], ALU.subtract).then_inc(m_d, 1)
                e.mark(v.memset(acc[:, :, :], 0.0))
                def look_onehot(j, at, used):
                    dve.wait_ge(k_tr[j], used)
                    build_onehot(onehot[j], col_lo[:, ds(at, U)]).then_inc(k_onehot[j], 1)

                look_onehot(0, U, l * (B_STEPS + 1))
                e.wait(dve)
                dve.sem_inc(dve_go, 1)
                with dve.Fori(0, B_STEPS) as b:
                    g = l * B_STEPS + b
                    for j in range(2):
                        n = g * 2 + (j + 1)
                        look_onehot(1 - j, (b * 4 + (2 * j + 3)) * U, [g, l * (B_STEPS + 1) + b + 1][j])
                        dve.wait_ge(k_edges[j], l * (B_STEPS + 1) + b + 1)
                        for q in range(2):
                            dve.wait_ge(k_rows[j][q], g + 1)
                            for k in range(U // 2):
                                i = q * (U // 2) + k
                                last = v.scalar_tensor_tensor(
                                    out=k_hot[:, i, 0:NB], in0=iota_b[:, 0:NB], scalar=k_edge[j][:, 1, i:i + 1],
                                    in1=bank_d[j][q][:, k, 0:NB], op0=ALU.is_equal, op1=ALU.mult,
                                    accum_out=k_d[j][:, 0, i:i + 1])
                            last.then_inc(k_sel[j][q], 1)
                        dve.wait_ge(k_sel[j][1], g + 1)
                        v.tensor_tensor(k_d[j][:, 1, :], k_d[j][:, 0, :], k_edge[j][:, 0, :], ALU.mult).then_inc(k_wd, 1)
                        build_onehot(k_hot, row_lo[:, ds((b * 4 + (2 * j + 1)) * U, U)]).then_inc(k_w, 1)
                        build_onehot(g_hot, row_lo[:, ds((b * 4 + 2 * j) * U, U)]).then_inc(g_w, 1)
                        for i, (summed, read, other, added) in enumerate((
                                (k_o[j], k_acc, g_acc, n - 1), (g_o[j], g_acc, k_acc, n))):
                            dve.load(blk, block_of[0:1, ds((b * 4 + (2 * j + 1 - i)) * U, 1)])
                            first = dve.snap(blk, min_val=0, max_val=BLOCKS - 1)
                            dve.wait_ge(summed, g + 1)
                            dve.wait_ge(other, added)
                            some = acc[:, ds(first, U), :].rearrange("p b d -> p (b d)")
                            v.tensor_tensor(some, some, bank[2 + i][:, :], ALU.add).then_inc(read, 1)
                dve.wait_ge(g_acc, (l + 1) * (2 * B_STEPS))
                dve.wait_ge(k_tr[0], (l + 1) * (B_STEPS + 1))
                dve.wait_ge(m_yst, (l + 1) * 16)
                v.tensor_tensor(x_cur[:, :, :], acc[:, 0:NB, :], d_wide, ALU.mult).then_inc(l_end, 1)
                dve.wait_ge(l_end, l * 2 + 1)
                v.tensor_tensor(total[:, :, :], total[:, :, :], x_cur[:, :, :], ALU.add).then_inc(l_end, 1)
                dve.wait_ge(l_end, l * 2 + 2)
            e = Steps(f_ch)
            wide = [PARTS, NB, HID]
            link(v.tensor_reduce(stat[:, 0, :], total[:, :, :], AX.X, ALU.add), e)
            link(v.tensor_scalar(stat[:, 3, :], stat[:, 0, :], 1.0 / HID, None, ALU.mult), e)
            link(v.tensor_tensor(total[:, :, :], total[:, :, :], stat[:, 3, :].unsqueeze(2).to_broadcast(wide),
                                 ALU.subtract), e)
            link(v.tensor_tensor(acc[:, 0:NB, :], total[:, :, :], total[:, :, :], ALU.mult), e)
            link(v.tensor_reduce(stat[:, 1, :], acc[:, 0:NB, :], AX.X, ALU.add), e)
            dve.wait_ge(f_sqrt, 1)
            link(v.reciprocal(stat[:, 0, :], stat[:, 2, :]), e)
            v.tensor_tensor(total[:, :, :], total[:, :, :], stat[:, 0, :].unsqueeze(2).to_broadcast(wide),
                            ALU.mult).then_inc(f_out, 1)


NAMES = {"x": "x", "src": "src", "dst": "dst", "L0_gnn_nb_W": "nb_W", "L0_gnn_nb_b": "nb_b",
         "L0_gnn_self_W": "self_W", "L0_gnn_self_b": "self_b", "L0_gnn_att1_W": "att1_W",
         "L0_gnn_att1_b": "att1_b", "L0_gnn_att2_W": "att2_W", "L0_gnn_att2_b": "att2_b"}


def kernel(**inputs):
    import numpy as np
    import concourse.bacc as bacc
    from concourse.bass_utils import run_bass_kernel_spmd

    nc = bacc.Bacc("TRN2", target_bir_lowering=False, num_devices=1)
    arrays, args = {}, {}
    for name, arg in NAMES.items():
        a = np.ascontiguousarray(inputs[name])
        arrays[f"in_{arg}"] = a
        args[arg] = nc.dram_tensor(f"in_{arg}", a.shape, mybir.dt.from_np(a.dtype), kind="ExternalInput").ap()
    shape = inputs["x"].shape
    args["out"] = nc.dram_tensor("out_0", shape, F32, kind="ExternalOutput").ap()
    build(nc, **args)
    r = run_bass_kernel_spmd(nc, [arrays], core_ids=[0])
    return r.results[0]["out_0"]
```

```python
import math
from contextlib import ExitStack

import concourse.bass as bass
from concourse import mybir

F32 = mybir.dt.float32
BF16 = mybir.dt.bfloat16
I32 = mybir.dt.int32
ALU = mybir.AluOpType
ACT = mybir.ActivationFunctionType
AX = mybir.AxisListType
ds = bass.ds

GAMMA, ZETA = -0.45, 1.05
PARTS = 128


def ceil_div(a, b):
    return -(-a // b)


class Steps:

    def __init__(self, sem, base=0):
        self.sem, self.base, self.n = sem, base, 0

    def mark(self, instruction):
        self.n += 1
        return instruction.then_inc(self.sem, 1)

    def wait(self, engine):
        engine.wait_ge(self.sem, self.base + self.n)


def build(nc, x, src, dst, nb_W, nb_b, self_W, self_b, att1_W, att1_b, att2_W, att2_b, out):
    NODES, HID = x.shape
    EDGES = src.shape[0]
    LAYERS = nb_W.shape[0]
    U = 8
    GRP = 4
    BLOCKS = ceil_div(NODES, PARTS)
    NODE_STEPS = ceil_div(BLOCKS, 2 * GRP)
    NB = NODE_STEPS * 2 * GRP
    PIECES = 8 if NB % 8 == 0 else 2
    FULL = NODES // PARTS
    LAST = NODES - FULL * PARTS
    EC = EDGES // PARTS
    EREST = EDGES - EC * PARTS
    SORT_STEPS = ceil_div(EC + (EREST > 0), 2 * U)
    ECP = SORT_STEPS * 2 * U
    EMPTY = ECP * PARTS - EDGES
    TILES = ceil_div(EDGES + BLOCKS * PARTS, 8 * U * PARTS) * 8 * U
    A_STEPS = TILES // (2 * U)
    QUADS = TILES // (4 * U)
    K_STEPS = 3 * QUADS
    B_BODIES = QUADS // 2
    AHEAD = 8 * U
    COL_GROUPS = ceil_div(TILES + AHEAD, PARTS)
    SLOTS = max(TILES, ceil_div(EDGES + (BLOCKS + 1) * PARTS + EMPTY, PARTS))
    NONE = BLOCKS + 1
    HIST_STEPS = ceil_div(BLOCKS, 2)
    TABLE = NB * PARTS

    def look_step(b, i):
        return b * 8 + (4 * (i // 3) + i % 3)

    ctx = ExitStack()
    with ctx:
        def sb(name, shape, dt):
            return ctx.enter_context(nc.sbuf_tensor(name, shape, dt))

        def sem(name):
            return ctx.enter_context(nc.semaphore(name))

        def two(name):
            return [sem(f"{name}{h}") for h in range(2)]

        slot_table = nc.dram_tensor("slot_table", (PARTS * SLOTS, 2), I32, kind="Internal").ap()
        qx_table = nc.dram_tensor("qx_table", (TABLE, 2 * HID), F32, kind="Internal").ap()
        y_table = nc.dram_tensor("y_table", (TABLE, HID), F32, kind="Internal").ap()
        kept_x = nc.dram_tensor("kept_x", (3 * QUADS * PARTS, U * HID), F32, kind="Internal").ap()
        col_rows = nc.dram_tensor("col_rows", (COL_GROUPS * PARTS, PARTS), BF16, kind="Internal").ap()

        qx_rows = qx_table.rearrange("(p b) d -> p b d", p=PARTS)

        iota_i = sb("iota_i", [PARTS, PARTS], I32)
        iota_b = sb("iota_b", [PARTS, PARTS], BF16)
        iota_f = sb("iota_f", [PARTS, PARTS], F32)
        part_i = sb("part_i", [PARTS, 1], I32)
        part_f = sb("part_f", [PARTS, 1], F32)
        upto = sb("upto", [PARTS, PARTS], BF16)
        after = sb("after", [PARTS, PARTS], BF16)
        before_f = sb("before_f", [PARTS, PARTS], F32)
        ident_b = sb("ident_b", [PARTS, PARTS], BF16)
        ident_f = sb("ident_f", [PARTS, PARTS], F32)
        zeros_b = sb("zeros_b", [PARTS, 512], BF16)
        real_b = sb("real_b", [PARTS, 1], BF16)
        real_t = sb("real_t", [PARTS, 1], F32)
        eps = sb("eps", [PARTS, 1], F32)
        one = sb("one", [PARTS, 1], F32)
        minus_part = sb("minus_part", [PARTS, 1], F32)

        x_cur = sb("x_cur", [PARTS, NB, HID], F32)
        total = sb("total", [PARTS, NB, HID], F32)
        acc = sb("acc", [PARTS, NB + U, HID], F32)
        p3 = sb("p3", [PARTS, NB * 3 * HID], BF16)
        p3v = p3[:, :].rearrange("p (b s d) -> p b s d", s=3, d=HID)
        d_node = sb("d_node", [PARTS, NB], F32)
        d3 = sb("d3", [PARTS, 3, NB], BF16)
        rows_sum = sb("rows_sum", [PARTS, NB], F32)
        stat = sb("stat", [PARTS, 4, NB], F32)

        row_lo = sb("row_lo", [PARTS, TILES + AHEAD], BF16)
        col_hi = sb("col_hi", [PARTS, TILES + AHEAD], F32)
        col_id = sb("col_id", [PARTS, TILES + AHEAD], I32)
        mask = sb("mask", [PARTS, TILES + AHEAD], F32)
        block_of = sb("block_of", [1, TILES + AHEAD], mybir.dt.int16)
        spot_of = sb("spot_of", [1, TILES], mybir.dt.int16)

        raw = p3[:, 0:4 * ECP].bitcast(I32).rearrange("p (w c) -> p w c", w=2)
        row_in = raw[:, 0, :]
        col_in = raw[:, 1, :]
        payload = p3[:, 4 * ECP:8 * ECP].bitcast(I32).rearrange("p (c w) -> p c w", w=2)
        bucket = p3[:, 8 * ECP:9 * ECP]
        acc_flat = acc[:, :, :].rearrange("p b d -> p (b d)")
        slots_in = acc_flat[:, 0:2 * SLOTS].bitcast(I32).rearrange("p (c w) -> p c w", w=2)
        started = acc_flat[:, 2 * SLOTS:2 * SLOTS + 256].bitcast(BF16)
        down = acc_flat[:, 2 * SLOTS + 256:2 * SLOTS + 256 + PARTS]
        band = acc_flat[:, 2 * SLOTS + 384:2 * SLOTS + 384 + PARTS].bitcast(BF16)
        hits = [acc_flat[:, 2 * SLOTS + 512 + h * ECP // 2:2 * SLOTS + 512 + (h + 1) * ECP // 2].bitcast(BF16)
                for h in range(2)]
        col_lo = p3[:, 0:COL_GROUPS * PARTS]
        col_turned = p3[:, COL_GROUPS * PARTS:2 * COL_GROUPS * PARTS].rearrange("p (i e) -> p i e", e=PARTS)
        col_tmp = x_cur[:, :, :].rearrange("p b d -> p (b d)")[:, 0:TILES].bitcast(I32)

        w_all = sb("w_all", [HID, LAYERS, 2 * HID], F32)
        bias_all = sb("bias_all", [2 * HID, LAYERS], F32)
        a1_all = sb("a1_all", [PARTS, LAYERS, 2 * HID], F32)
        b1_all = sb("b1_all", [PARTS, LAYERS, HID], F32)
        a2_all = sb("a2_all", [PARTS, LAYERS, HID], F32)
        b2_all = sb("b2_all", [PARTS, LAYERS], F32)
        w_cur = sb("w_cur", [HID, 2 * HID], F32)
        bias_cur = sb("bias_cur", [2 * HID, 1], F32)
        a1_cur = sb("a1_cur", [PARTS, 2 * HID], F32)
        b1_cur = sb("b1_cur", [PARTS, HID], F32)
        a2_cur = sb("a2_cur", [PARTS, HID], F32)
        b2_cur = sb("b2_cur", [PARTS, 1], F32)

        def ring(name, shape, dt):
            return [sb(f"{name}{h}", shape, dt) for h in range(2)]

        onehot = ring("onehot", [PARTS, U, PARTS], BF16)
        onehot_t = ring("onehot_t", [PARTS, U, PARTS], BF16)
        index = ring("index", [PARTS, U], I32)
        pay = ring("pay", [PARTS, U, 2], I32)
        got = ring("got", [PARTS, U, 2 * HID], F32)
        hidden = ring("hidden", [PARTS, U, HID], F32)
        small = ring("small", [PARTS, 8, U], F32)
        small_i = ring("small_i", [PARTS, 3, U], I32)
        mask3 = ring("mask3", [PARTS, U, 3], BF16)
        rank_f = ring("rank_f", [PARTS, U], F32)
        junk = sb("junk", [PARTS, PARTS], F32)
        g_hot = sb("g_hot", [PARTS, U, PARTS], F32)
        k_weight = ring("k_weight", [PARTS, 2, U], F32)
        taken = [0]

        def in_p3(shape, dt):
            n = math.prod(shape) * (2 if dt == F32 else 1)
            flat = p3[:, taken[0]:taken[0] + n]
            taken[0] += n
            flat = flat.bitcast(F32) if dt == F32 else flat
            return flat.rearrange("p (k m) -> p k m", m=shape[1])

        k_hot = [sb("k_hot0", [PARTS, U, PARTS], F32), in_p3([U, PARTS], F32)]
        k_cols = [in_p3([U, PARTS], BF16) for _ in range(3)]
        k_far = in_p3([U, PARTS], BF16)
        picked = in_p3([U, NB], F32)
        k_x = [sb("k_x0", [PARTS, U, HID], F32), sb("k_x1", [PARTS, U, HID], F32), in_p3([U, HID], F32)]
        x_t = [g_hot[0:HID, h * GRP:(h + 1) * GRP, :].rearrange("p g m -> p (g m)") for h in range(2)]
        f_t = [k_hot[0][:, h * GRP:(h + 1) * GRP, :].rearrange("p g m -> p (g m)") for h in range(2)]
        x_step = ring("x_step", [PARTS, GRP, HID], F32)
        q_step = ring("q_step", [PARTS, GRP, HID], F32)
        rest = [hidden[h][:, :, :].rearrange("p (w g) d -> p w g d", w=2) for h in range(2)]
        cnt = sb("cnt", [PARTS, 4], F32)
        cnt_i = sb("cnt_i", [PARTS, 2], I32)
        cnt_w = sb("cnt_w", [PARTS, PARTS], F32)

        bank = [ctx.enter_context(nc.psum_tensor(f"bank{i}", [PARTS, 512], F32)) for i in range(8)]
        bank_t = [bank[h][:, :].bitcast(BF16).rearrange("p (k m) -> p k m", k=U) for h in range(2)]
        bank_p = [bank[2 + h][:, :].rearrange("p (k d) -> p k d", k=U) for h in range(2)]
        bank_r = bank[6]
        bank_s = bank[4]
        bank_d = [[bank[4 + 2 * j + q][:, :].rearrange("p (k m) -> p k m", k=U // 2) for q in range(2)]
                  for j in range(2)]

        s_rows, s_load = sem("s_rows"), sem("s_load")
        pool_go, pe_go, dve_go, sp_go = sem("pool_go"), sem("pe_go"), sem("dve_go"), sem("sp_go")
        s_iota, s_const, s_open, s_fillsrc, s_fill = (
            sem("s_iota"), sem("s_const"), sem("s_open"), sem("s_fillsrc"), sem("s_fill"))
        s_edges_in = sem("s_edges_in")
        s_chain, s_hits, s_hitsum = sem("s_chain"), two("s_hits"), two("s_hitsum")
        s_hist, s_tiles, s_starts, s_blk, s_blkuse = (
            sem("s_hist"), sem("s_tiles"), sem("s_starts"), sem("s_blk"), sem("s_blkuse"))
        s_pay, s_onehot, s_rank, s_pick, s_rest, s_idx, s_scat = (
            two("s_pay"), two("s_onehot"), two("s_rank"), two("s_pick"), two("s_rest"), two("s_idx"), two("s_scat"))
        s_slot = sem("s_slot")
        s_back, s_edges = sem("s_back"), sem("s_edges")
        t_turn, t_copy, t_table = sem("t_turn"), sem("t_copy"), sem("t_table")
        n_cur = sem("n_cur")
        n_x, n_xt, n_xtc, n_f, n_fc, n_pq, n_q, n_qst = (
            two("n_x"), two("n_xt"), two("n_xtc"), two("n_f"), two("n_fc"), two("n_pq"), two("n_q"), two("n_qst"))
        n_ch, n_xst = sem("n_ch"), sem("n_xst")
        a_idx, a_got, a_kept, a_onehot, a_tr, a_trc, a_p, a_add, a_sum, a_sig, a_m3, a_row = (
            two("a_idx"), two("a_got"), two("a_kept"), two("a_onehot"), two("a_tr"), two("a_trc"), two("a_p"),
            two("a_add"), two("a_sum"), two("a_sig"), two("a_m3"), two("a_row"))
        a_ch = sem("a_ch")
        m_rows, m_ch, m_sqrt, m_d, m_y, m_yst = (
            sem("m_rows"), sem("m_ch"), sem("m_sqrt"), sem("m_d"), sem("m_y"), sem("m_yst"))
        g_idx, g_got, g_w, g_o, g_acc = two("g_idx"), two("g_got"), sem("g_w"), two("g_o"), sem("g_acc")
        k_colin, k_xin, k_o = ([sem(f"{name}{c}") for c in range(3)] for name in ("k_colin", "k_xin", "k_o"))
        k_away = sem("k_away")
        k_onehot = [sem("k_onehot_dve"), sem("k_onehot_act")]
        k_rows, k_sel, k_wt, k_w, k_xs, g_xs, k_acc = (
            sem("k_rows"), sem("k_sel"), sem("k_wt"), sem("k_w"), sem("k_xs"), sem("g_xs"),
            two("k_acc"))
        l_end = sem("l_end")
        f_ch, f_mid, f_sq, f_var, f_sqrt, f_out, f_done = (
            sem("f_ch"), sem("f_mid"), sem("f_sq"), sem("f_var"), sem("f_sqrt"), sem("f_out"), sem("f_done"))

        ROW_LOADS = 16 * (1 + (EREST > 0))
        loads = [0]
        GOT = 16 * U

        def piece(c):
            return slice(c * (NB // PIECES), (c + 1) * (NB // PIECES))

        def summed(l, b, i):
            c = i % 3
            return k_o[c], l * (QUADS + (c == 2)) + (b * 2 + (i // 3 + 1 + (c == 2)))

        def joined(l, b, i):
            h = i % 2
            return k_acc[h], l * (K_STEPS // 2 + h) + (b * 3 + (i // 2 + 1 + h))

        def turned(l, b, i):
            c = i % 3
            if c == 0:
                return k_onehot[0], l * (QUADS + 1) + (b * 2 + (i // 3 + 1))
            return k_onehot[1], l * (2 * QUADS + 1) + (b * 4 + (2 * (i // 3) + c))

        def columns_in(l, b, i):
            return k_colin[i % 3], (l * (QUADS + (i % 3 < 2)) + b * 2 + (i // 3 + 1)) * 16

        block = ctx.enter_context(nc.Block())

        @block.sync
        def _(sp):
            def load(to, of):
                loads[0] += 16
                sp.dma_start(to, of).then_inc(s_load, 16)

            sp.wait_ge(s_open, 1)
            for to, of, signal in ((row_in, src, s_rows), (col_in, dst, s_load)):
                sp.dma_start(to[:, 0:EC], of[0:EC * PARTS].rearrange("(p c) -> p c", c=EC)).then_inc(signal, 16)
                if EREST:
                    sp.dma_start(to[0:EREST, EC:EC + 1],
                                 of[EC * PARTS:EDGES].rearrange("(p c) -> p c", c=1)).then_inc(signal, 16)
            loads[0] += ROW_LOADS
            sp.wait_ge(s_fillsrc, 1)
            sp.dma_start(slot_table.rearrange("(p c) w -> p c w", c=SLOTS), slots_in).then_inc(s_fill, 16)
            load(total[:, 0:FULL, :], x[0:FULL * PARTS, :].rearrange("(b p) d -> p b d", p=PARTS))
            if LAST:
                load(total[0:LAST, FULL, :], x[FULL * PARTS:NODES, :])
            load(w_all[:, :, 0:HID], nb_W.rearrange("l k m -> k l m"))
            load(w_all[:, :, HID:2 * HID], self_W.rearrange("l k m -> k l m"))
            load(a1_all[0:HID, :, 0:HID], att1_W[:, 0:HID, :].rearrange("l k m -> k l m"))
            load(a1_all[HID:2 * HID, :, HID:2 * HID], att1_W[:, HID:2 * HID, :].rearrange("l k m -> k l m"))
            with nc.allow_non_contiguous_dma(reason="a few hundred biases"):
                for l in range(LAYERS):
                    load(bias_all[0:HID, l:l + 1], nb_b[l].rearrange("(p c) -> p c", c=1))
                    load(bias_all[HID:2 * HID, l:l + 1], self_b[l].rearrange("(p c) -> p c", c=1))
            load(b1_all[:, :, :], att1_b.partition_broadcast(PARTS))
            load(a2_all[:, :, :], att2_W.rearrange("l k o -> l (k o)").partition_broadcast(PARTS))
            load(b2_all[:, :], att2_b.rearrange("l o -> (l o)").partition_broadcast(PARTS))
            for h in range(2):
                sp.wait_ge(s_scat[h], GOT * SORT_STEPS)
            sp.dma_start(slots_in, slot_table.rearrange("(p c) w -> p c w", c=SLOTS)).then_inc(s_back, 16)
            sp.wait_ge(t_copy, COL_GROUPS)
            sp.dma_start(col_rows.rearrange("(i t) e -> t i e", t=PARTS), col_turned).then_inc(t_table, 16)
            with sp.Fori(0, LAYERS) as l:
                sp.wait_ge(n_cur, l + 1)
                sp.dma_start(qx_rows[:, :, HID:2 * HID],
                             x_cur[:, :, :]).then_inc(n_xst, 16)
                sp.sem_inc(sp_go, 1)
                with sp.Fori(0, NODE_STEPS) as b:
                    for h in range(2):
                        sp.wait_ge(n_q[h], l * NODE_STEPS + b + 1)
                        sp.dma_start(qx_rows[:, ds((b * 2 + h) * GRP, GRP), 0:HID], q_step[h][:, :, :]).then_inc(n_qst[h], 16)
                with sp.Fori(0, QUADS) as b:
                    for j in range(3):
                        sp.wait_ge(a_got[j % 2], (l * A_STEPS + b * 2 + (j // 2 + 1)) * GOT)
                        sp.sem_inc(sp_go, 1)
                        sp.dma_start(kept_x[ds((b * 3 + j) * PARTS, PARTS), :].rearrange("p (k d) -> p k d", k=U),
                                     got[j % 2][:, :, HID:2 * HID]).then_inc(a_kept[j % 2], 16)
                sp.wait_ge(m_y, l + 1)
                sp.dma_start(y_table.rearrange("(p b) d -> p b d", p=PARTS), x_cur[:, :, :]).then_inc(m_yst, 16)
                for h in range(2):
                    sp.wait_ge(a_kept[h], (l + 1) * (16 * [2 * QUADS, QUADS][h]))
                    sp.sem_inc(sp_go, 1)

                def load_columns(c, at):
                    sp.dma_start(k_cols[c], col_rows[ds(at, U), :].rearrange("t e -> (t e)")
                                 .partition_broadcast(PARTS).rearrange("p (t e) -> p t e", e=PARTS)).then_inc(k_colin[c], 16)

                sp.wait_ge(t_table, 16)
                for i in range(2):
                    load_columns(i, i * U)
                sp.sem_inc(sp_go, 1)
                with sp.Fori(0, B_BODIES) as b:
                    for i in range(6):
                        sp.wait_ge(k_sel, l * (2 * (K_STEPS + 1)) + (b * 6 + i) * 2)
                        sp.sem_inc(sp_go, 1)
                        load_columns((i + 2) % 3, look_step(b, i + 2) * U)
                        sp.wait_ge(*summed(l, b, i - 3))
                        sp.sem_inc(sp_go, 1)
                        sp.dma_start(k_x[i % 3][:, :, :], kept_x[ds((b * 6 + i) * PARTS, PARTS), :]
                                     .rearrange("p (k d) -> p k d", k=U)).then_inc(k_xin[i % 3], 16)
            done = 0
            for c in range(PIECES):
                first, end = piece(c).start, min(piece(c).stop, FULL)
                sp.wait_ge(f_out, c + 1)
                if first < end:
                    sp.dma_start(out[first * PARTS:end * PARTS, :].rearrange("(b p) d -> p b d", p=PARTS),
                                 total[:, first:end, :]).then_inc(f_done, 16)
                    done += 16
                if LAST and piece(c).start <= FULL < piece(c).stop:
                    sp.dma_start(out[FULL * PARTS:NODES, :], total[0:LAST, FULL, :]).then_inc(f_done, 16)
                    done += 16
            sp.wait_ge(f_done, done)

        @block.gpsimd
        def _(pool):
            pool.iota(iota_i[:, :], [[1, PARTS]], base=0, channel_multiplier=0).then_inc(s_iota, 1)
            pool.iota(part_i[:, :], [[0, 1]], base=0, channel_multiplier=1).then_inc(s_iota, 1)
            pool.wait_ge(s_fill, 16)
            with pool.Fori(0, SORT_STEPS) as g:
                for h in range(2):
                    pool.wait_ge(s_pay[h], g + 1)
                    pool.wait_ge(s_idx[h], g + 1)
                    pool.sem_inc(pool_go, 1)
                    for k in range(U):
                        pool.indirect_dma_start(
                            slot_table, bass.IndirectOffsetOnAxis(ap=index[h][:, k:k + 1], axis=0),
                            pay[h][:, k, :], None).then_inc(s_scat[h], 16)
            with pool.Fori(0, LAYERS) as l:
                pool.wait_ge(n_cur, l + 1)
                pool.sem_inc(pool_go, 1)
                with pool.Fori(0, NODE_STEPS) as b:
                    n = l * NODE_STEPS + b
                    for h in range(2):
                        pool.wait_ge(n_xt[h], n)
                        pool.sem_inc(pool_go, 1)
                        pool.tensor_copy(x_step[h][:, :, :],
                                         x_cur[:, ds((b * 2 + h) * GRP, GRP), :]).then_inc(n_x[h], 1)
                for h in range(2):
                    pool.wait_ge(n_qst[h], (l + 1) * (16 * NODE_STEPS))
                pool.wait_ge(n_xst, (l + 1) * 16)
                pool.sem_inc(pool_go, 1)
                with pool.Fori(0, QUADS) as b:
                    for j in range(4):
                        h = j % 2
                        g = l * A_STEPS + (b * 2 + j // 2)
                        pool.wait_ge(a_idx[h], l * (A_STEPS + 1) + (b * 2 + (j // 2 + 1)))
                        pool.wait_ge(a_add[h], g)
                        if j != 1:
                            pool.wait_ge(a_kept[h], (g if h == 0 else l * QUADS + b + 1) * 16)
                        pool.sem_inc(pool_go, 1)
                        for k in range(U):
                            pool.indirect_dma_start(
                                got[h][:, k, :], None, qx_table,
                                bass.IndirectOffsetOnAxis(ap=index[h][:, k:k + 1], axis=0)
                            ).then_inc(a_got[h], 16)
                for h in range(2):
                    pool.wait_ge(a_kept[h], (l + 1) * (16 * [2 * QUADS, QUADS][h]))
                pool.wait_ge(m_yst, (l + 1) * 16)
                pool.sem_inc(pool_go, 1)
                with pool.Fori(0, B_BODIES) as b:
                    for j in range(2):
                        pool.wait_ge(g_idx[j], l * (B_BODIES + 1) + b + 1)
                        pool.wait_ge(g_o[j], l * B_BODIES + b)
                        pool.sem_inc(pool_go, 1)
                        for k in range(U):
                            pool.indirect_dma_start(
                                got[j][:, k, 0:HID], None, y_table,
                                bass.IndirectOffsetOnAxis(ap=index[j][:, k:k + 1], axis=0)
                            ).then_inc(g_got[j], 16)

        @block.tensor
        def _(pe):
            mm = nc.tensor.matmul
            turn = nc.tensor.transpose

            def plus(to, lhsT, rhs):
                return mm(to, lhsT, rhs, start=False, stop=True, skip_group_check=True)

            pe.wait_ge(s_const, 1)
            mm(bank[5][:, :], zeros_b[:, 0:PARTS], zeros_b[:, :], start=True, stop=True, skip_group_check=True)
            with pe.Fori(0, HIST_STEPS) as b:
                for h in range(2):
                    pe.wait_ge(s_hits[h], b + 1)
                    for at in range(0, ECP, 512):
                        w = min(512, ECP - at)
                        last = plus(bank[5][:, 0:w], band[:, ds(b * 2 + (PARTS - 2 * HIST_STEPS + h), PARTS)],
                                    hits[h][:, at:at + w])
                    last.then_inc(s_hitsum[h], 1)
            plus(bank[5][:, 0:8], zeros_b[:, 0:PARTS], zeros_b[:, 0:8]).then_inc(s_hist, 1)
            pe.wait_ge(s_tiles, 1)
            mm(bank[7][:, 0:1], before_f[:, :], cnt[:, 1:2], start=True, stop=True).then_inc(s_starts, 1)
            mm(bank_s[:, 0:PARTS], cnt_w[:, :], before_f[:, :], start=True, stop=True, skip_group_check=True)
            with pe.Fori(0, SORT_STEPS) as g:
                for h in range(2):
                    pe.wait_ge(s_onehot[h], g + 1)
                    for k in range(U):
                        plus(bank_s[:, 0:PARTS], upto[:, :], onehot[h][:, k, :]).then_inc(s_rank[h], 1)
                        pe.wait_ge(s_pick[h], g * U + (k + 1))
                        plus(bank_s[:, 0:PARTS], after[:, :], onehot[h][:, k, :]).then_inc(s_rest[h], 1)
            for c, at in enumerate(range(0, TILES, 512)):
                w = min(512, TILES - at)
                pe.wait_ge(s_blk, c + 1)
                mm(bank[5][0:1, 0:w], real_b[:, :], started[:, 0:w], start=True, stop=True).then_inc(s_blkuse, 1)
            pe.wait_ge(s_edges, 1)
            for i in range(COL_GROUPS):
                if i >= 2:
                    pe.wait_ge(t_copy, i - 1)
                turn(bank_t[i % 2][:, 0, :], col_lo[:, i * PARTS:(i + 1) * PARTS], ident_b[:, :]).then_inc(t_turn, 1)
            blk = [pe.alloc_register(f"pe_blk{k}") for k in range(U)]

            with pe.Fori(0, LAYERS) as l:
                pe.wait_ge(n_cur, l + 1)
                pe.sem_inc(pe_go, 1)
                with pe.Fori(0, NODE_STEPS) as b:
                    n = l * NODE_STEPS + b
                    for h in range(2):
                        pe.wait_ge(n_x[h], n + 1)
                        pe.sem_inc(pe_go, 1)
                        for i in range(GRP):
                            last = turn(bank[h][0:HID, i * PARTS:(i + 1) * PARTS], x_step[h][:, i, :],
                                        ident_f[:, :])
                        last.then_inc(n_xt[h], 1)
                    for h in range(2):
                        pe.wait_ge(n_xtc[h], n + 1)
                        mm(bank[2 + h][:, :], w_cur[:, :], x_t[h], start=True, stop=True).then_inc(n_f[h], 1)
                    for h in range(2):
                        pe.wait_ge(n_fc[h], n + 1)
                        pe.wait_ge(n_q[h], n)
                        for i in range(GRP):
                            last = mm(bank[4 + h][:, i * PARTS:(i + 1) * PARTS], f_t[h][:, i * PARTS:(i + 1) * PARTS],
                                      a1_cur[:, :], start=True, stop=True)
                        last.then_inc(n_pq[h], 1)
                mm(bank_r[:, :], zeros_b[:, 0:PARTS], zeros_b[:, :], start=True, stop=True, skip_group_check=True)

                def spread(h, at, used, read):
                    pe.load(blk, block_of[0:1, ds(at, U)])
                    ids = [pe.snap(r, min_val=0, max_val=BLOCKS - 1) for r in blk]
                    pe.wait_ge(a_onehot[h], used + 1)
                    for k in range(U):
                        last = turn(bank_t[h][:, k, :], onehot[h][:, k, :], ident_b[:, :])
                    last.then_inc(a_tr[h], 1)
                    pe.wait_ge(a_trc[h], used + 1)
                    pe.wait_ge(a_add[h], read)
                    for k in range(U):
                        for s in range(3):
                            last = mm(bank_p[h][:, k, :], onehot_t[h][:, k, :],
                                      p3v[:, ds(ids[k], 1), s, :].rearrange("p o d -> p (o d)"),
                                      start=(s == 0), stop=(s == 2))
                    last.then_inc(a_p[h], 1)

                spread(0, 0, l * (A_STEPS + 1), l * A_STEPS)
                with pe.Fori(0, A_STEPS) as b:
                    g = l * A_STEPS + b
                    for h in range(2):
                        spread(1 - h, (b * 2 + (h + 1)) * U, [g, l * (A_STEPS + 1) + b + 1][h], g + h)
                        pe.load(blk, block_of[0:1, ds((b * 2 + h) * U, U)])
                        at = [pe.snap(r, min_val=0, max_val=BLOCKS - 1) for r in blk]
                        pe.wait_ge(a_m3[h], g + 1)
                        for k in range(U):
                            last = plus(bank_r[:, ds(at[k] * 4, 3)], onehot[h][:, k, :], mask3[h][:, k, :])
                        last.then_inc(a_row[h], 1)
                plus(bank_r[:, 0:4], zeros_b[:, 0:PARTS], zeros_b[:, 0:4]).then_inc(m_rows, 1)

                def pick_rows(b, i):
                    j, k = i % 2, b * 6 + i
                    pe.wait_ge(*turned(l, b, i))
                    for q in range(2):
                        if not isinstance(k, int):
                            pe.wait_ge(k_sel, l * (2 * (K_STEPS + 1)) + (k - 2) * 2 + (q + 1))
                        for i in range(U // 2):
                            for s in range(3):
                                last = mm(bank_d[j][q][:, i, 0:NB], onehot_t[j][:, q * (U // 2) + i, :],
                                          d3[:, s, :], start=(s == 0), stop=(s == 2))
                        last.then_inc(k_rows, 1)

                def sum_edges(to, hot, rows, at, ready, half):
                    mm(to[:, :], zeros_b[:, 0:PARTS], zeros_b[:, :], start=True, stop=True, skip_group_check=True)
                    for k in range(U):
                        if k % (U // 2) == 0:
                            pe.wait_ge(ready, half + (k // (U // 2) + 1))
                        last = plus(to[:, ds(at[k], HID)], hot[:, k, :], rows[:, k, 0:HID])
                    return last

                def spots(at):
                    pe.load(blk, spot_of[0:1, ds(at, U)])
                    return [pe.snap(r, min_val=0, max_val=(U - 1) * HID) for r in blk]

                pe.wait_ge(m_d, l + 1)
                for j in range(2):
                    pick_rows(0, j)
                mm(bank[2][:, :], zeros_b[:, 0:PARTS], zeros_b[:, :], start=True, stop=True,
                   skip_group_check=True).then_inc(k_o[2], 1)
                with pe.Fori(0, B_BODIES) as b:
                    for i in range(6):
                        k = b * 6 + i
                        at = spots(look_step(b, i) * U)
                        pe.wait_ge(*joined(l, b, i - 2))
                        pe.wait_ge(k_w, l * (K_STEPS + 1) + k + 1)
                        sum_edges(bank[1 + i % 2], k_hot[i % 2], k_x[i % 3], at, k_xs,
                                  (l * K_STEPS + k) * 2).then_inc(k_o[i % 3], 1)
                        pick_rows(b, i + 2)
                        if i % 3 == 1:
                            m = l * QUADS + (b * 2 + i // 3)
                            at = spots((b * 8 + (4 * (i // 3) + 3)) * U)
                            pe.wait_ge(g_acc, m)
                            pe.wait_ge(g_w, m + 1)
                            sum_edges(bank[3], g_hot, got[i // 3], at, g_xs, m * 2).then_inc(g_o[i // 3], 1)
                pe.sem_inc(pe_go, 1)

        @block.scalar
        def _(act):
            a = nc.scalar
            act.wait_ge(s_edges_in, 1)
            with act.Fori(0, SORT_STEPS) as g:
                for h in range(2):
                    act.wait_ge(s_scat[h], g * GOT)
                    a.copy(pay[h][:, :, :], payload[:, ds((g * 2 + h) * U, U), :]).then_inc(s_pay[h], 1)
            for i in range(COL_GROUPS):
                act.wait_ge(t_turn, i + 1)
                a.copy(col_turned[:, i, :], bank_t[i % 2][:, 0, :]).then_inc(t_copy, 1)
            act.wait_ge(s_edges, 1)
            with act.Fori(0, LAYERS) as l:
                with act.Fori(0, NODE_STEPS) as b:
                    n = l * NODE_STEPS + b
                    for h in range(2):
                        act.wait_ge(n_xt[h], n + 1)
                        a.copy(x_t[h], bank[h][0:HID, :]).then_inc(n_xtc[h], 1)
                    for h in range(2):
                        act.wait_ge(n_f[h], n + 1)
                        act.wait_ge(n_pq[h], n)
                        a.activation(f_t[h], bank[2 + h][:, :], ACT.Relu, bias=bias_cur[:, :]).then_inc(n_fc[h], 1)
                for h in range(2):
                    act.wait_ge(g_idx[h], l * (B_BODIES + 1))
                    a.copy(index[h][:, :], col_id[:, h * U:(h + 1) * U]).then_inc(a_idx[h], 1)

                def spread_turned(h, used):
                    act.wait_ge(a_tr[h], used + 1)
                    act.wait_ge(a_p[h], used)
                    a.copy(onehot_t[h][:, :, :], bank_t[h]).then_inc(a_trc[h], 1)

                spread_turned(0, l * (A_STEPS + 1))
                with act.Fori(0, A_STEPS) as b:
                    g = l * A_STEPS + b
                    for h in range(2):
                        spread_turned(1 - h, [g, l * (A_STEPS + 1) + b + 1][h])
                        act.wait_ge(a_sum[h], g + 1)
                        a.activation(small[h][:, 1, :], small[h][:, 7, :], ACT.Exp, scale=-1.0).then_inc(a_sig[h], 1)
                        act.wait_ge(a_got[h], (g + 1) * GOT)
                        a.copy(index[h][:, :], col_id[:, ds((b * 2 + 2 + h) * U, U)]).then_inc(a_idx[h], 1)
                act.wait_ge(m_ch, l * 7 + 2)
                a.activation(stat[:, 0, :], rows_sum[:, :], ACT.Sqrt).then_inc(m_sqrt, 1)

                for j in range(2):
                    act.wait_ge(a_idx[j], (l + 1) * (A_STEPS + 1))
                    a.copy(index[j][:, :], col_id[:, (4 * j + 3) * U:(4 * j + 4) * U]).then_inc(g_idx[j], 1)

                def scale_rows(rows, by, signal):
                    for k in range(U):
                        last = a.activation(rows[:, k, 0:HID], rows[:, k, 0:HID], ACT.Copy, scale=by(k))
                        if k % (U // 2) == U // 2 - 1:
                            last.then_inc(signal, 1)

                def look_onehot(b, i):
                    c, j, k = i % 3, i % 2, b * 6 + i
                    sem, n = turned(l, b, i)
                    act.wait_ge(*columns_in(l, b, i))
                    act.wait_ge(sem, n - 1)
                    a.activation(k_far, k_cols[c], ACT.Abs, bias=minus_part[:, :]).then_inc(k_away, 1)
                    if not isinstance(k, int):
                        act.wait_ge(k_rows, l * (2 * (K_STEPS + 2)) + (k - 1) * 2)
                    act.wait_ge(k_away, n)
                    a.activation(onehot_t[j][:, :, :], k_far, ACT.Relu, bias=one[:, :], scale=-1.0).then_inc(sem, 1)

                look_onehot(0, 1)
                with act.Fori(0, B_BODIES) as b:
                    for i in range(6):
                        if i % 3 != 1:
                            look_onehot(b, i + 2)
                        act.wait_ge(k_xin[i % 3], (l * QUADS + (b * 2 + (i // 3 + 1))) * 16)
                        act.wait_ge(k_wt, l * (K_STEPS + 1) + b * 6 + (i + 1))
                        scale_rows(k_x[i % 3], lambda k: k_weight[i % 2][:, 1, k:k + 1], k_xs)
                        if i % 3 != 1:
                            continue
                        j = i // 3
                        act.wait_ge(g_got[j], (l * B_BODIES + b + 1) * GOT)
                        scale_rows(got[j], lambda k: mask[:, ds((b * 8 + (4 * j + 3)) * U + k, 1)], g_xs)
                        a.copy(index[j][:, :], col_id[:, ds((b * 8 + (4 * j + 11)) * U, U)]).then_inc(g_idx[j], 1)
            for c in range(PIECES):
                some = piece(c)
                act.wait_ge(f_mid, c + 1)
                a.activation(acc[:, some, :], total[:, some, :], ACT.Square).then_inc(f_sq, 1)
                act.wait_ge(f_var, c + 1)
                a.activation(stat[:, 2, some], stat[:, 1, some], ACT.Sqrt, bias=eps[:, :],
                             scale=1.0 / HID).then_inc(f_sqrt, 1)

        @block.vector
        def _(dve):
            v = nc.vector
            c = Steps(s_chain)
            shift = PARTS.bit_length() - 1

            def link(instruction, steps=None):
                (steps or c).mark(instruction)
                (steps or c).wait(dve)

            v.memset(row_in[:, EC:ECP], NONE * PARTS)
            v.memset(col_in[:, EC:ECP], 0)
            v.memset(total[:, FULL:NB, :], 0.0)
            v.memset(a1_all[:, :, :], 0.0).then_inc(s_open, 1)
            v.memset(slots_in[:, :, 0], PARTS)
            v.memset(slots_in[:, :, 1], 0).then_inc(s_fillsrc, 1)
            v.memset(zeros_b[:, :], 0.0)
            v.memset(eps[:, :], 1e-5)
            v.memset(one[:, :], 1.0)
            v.memset(band[:, 0:PARTS - 1], 0.0)
            v.memset(band[:, PARTS - 1:PARTS], 1.0)
            v.memset(band[:, PARTS:2 * PARTS], 0.0)
            for edges in (row_lo, col_hi, col_id, mask):
                v.memset(edges[:, TILES:TILES + AHEAD], 0)
            dve.wait_ge(s_iota, 2)
            v.tensor_copy(iota_b[:, :], iota_i[:, :])
            v.tensor_copy(iota_f[:, :], iota_i[:, :])
            link(v.tensor_copy(part_f[:, :], part_i[:, :]))
            v.tensor_scalar(minus_part[:, :], part_f[:, :], -1.0, None, ALU.mult)
            v.tensor_scalar(down, iota_f[:, :], -1.0, float(PARTS - 1), ALU.mult, ALU.add)
            v.tensor_scalar(upto[:, :], iota_f[:, :], part_f[:, :], None, ALU.is_ge)
            v.tensor_scalar(after[:, :], iota_f[:, :], part_f[:, :], None, ALU.is_lt)
            v.tensor_scalar(before_f[:, :], iota_f[:, :], part_f[:, :], None, ALU.is_gt)
            v.tensor_scalar(ident_b[:, :], iota_f[:, :], part_f[:, :], None, ALU.is_equal)
            v.tensor_scalar(ident_f[:, :], iota_f[:, :], part_f[:, :], None, ALU.is_equal)
            link(v.tensor_scalar(real_t[:, :], part_f[:, :], 0.5, None, ALU.is_gt))
            v.scalar_tensor_tensor(out=real_b[:, :], in0=part_f[:, :], scalar=float(BLOCKS) - 0.5,
                                   in1=real_t[:, :], op0=ALU.is_lt, op1=ALU.mult).then_inc(s_const, 1)
            dve.wait_ge(s_rows, ROW_LOADS)
            v.tensor_scalar(payload[:, :, 0], row_in, PARTS - 1, None, ALU.bitwise_and)
            link(v.tensor_scalar(row_in, row_in, shift, None, ALU.logical_shift_right))
            link(v.tensor_copy(bucket, row_in))
            with dve.Fori(0, HIST_STEPS) as b:
                for h in range(2):
                    dve.wait_ge(s_hitsum[h], b)
                    v.tensor_scalar(hits[h], bucket, down[:, ds(b * 2 + (PARTS - 2 * HIST_STEPS + h), 1)], None,
                                    ALU.is_equal).then_inc(s_hits[h], 1)
            dve.wait_ge(s_load, loads[0])
            v.tensor_copy(payload[:, :, 1], col_in)
            link(v.tensor_scalar(row_in, row_in, NONE, None, ALU.is_equal))
            v.scalar_tensor_tensor(out=payload[:, :, 0], in0=row_in, scalar=float(PARTS), in1=payload[:, :, 0],
                                   op0=ALU.mult, op1=ALU.add).then_inc(s_edges_in, 1)
            dve.wait_ge(s_hist, 1)
            link(v.tensor_reduce(cnt[:, 0:1], bank[5][:, :], AX.X, ALU.add))
            link(v.tensor_scalar(cnt_i[:, 0:1], cnt[:, 0:1], float(PARTS - 1), None, ALU.add))
            link(v.tensor_scalar(cnt_i[:, 1:2], cnt_i[:, 0:1], shift, None, ALU.logical_shift_right))
            link(v.tensor_scalar(cnt[:, 1:2], cnt_i[:, 1:2], 1.0, None, ALU.max))
            link(v.tensor_scalar(cnt[:, 2:3], cnt[:, 1:2], float(PARTS), None, ALU.mult))
            v.tensor_copy(cnt_w[:, :], cnt[:, 2:3].to_broadcast([PARTS, PARTS])).then_inc(s_tiles, 1)

            def build_onehot(to, of):
                wide = [PARTS, U, PARTS]
                return v.tensor_tensor(to[:, :, :], iota_b[:, :].unsqueeze(1).to_broadcast(wide),
                                       of.unsqueeze(2).to_broadcast(wide), ALU.is_equal)

            with dve.Fori(0, SORT_STEPS) as g:
                for h in range(2):
                    dve.wait_ge(s_rest[h], g * U)
                    build_onehot(onehot[h], bucket[:, ds((g * 2 + h) * U, U)]).then_inc(s_onehot[h], 1)
                    dve.wait_ge(s_onehot[h], g + 1)
                    for k in range(U):
                        dve.wait_ge(s_rank[h], g * U + (k + 1))
                        v.tensor_tensor_reduce(out=junk[:, :], in0=bank_s[:, 0:PARTS], in1=onehot[h][:, k, :],
                                               scale=1.0, scalar=0.0, op0=ALU.mult, op1=ALU.add,
                                               accum_out=rank_f[h][:, k:k + 1]).then_inc(s_pick[h], 1)
                    dve.wait_ge(s_pick[h], (g + 1) * U)
                    e = Steps(s_slot, (g * 2 + h) * 2)
                    i = small_i[h]
                    link(v.tensor_scalar(i[:, 0, :], rank_f[h][:, :], -1.0, None, ALU.add), e)
                    v.tensor_scalar(i[:, 1, :], i[:, 0, :], PARTS - 1, None, ALU.bitwise_and)
                    link(v.tensor_scalar(i[:, 2, :], i[:, 0, :], shift, None, ALU.logical_shift_right), e)
                    dve.wait_ge(s_scat[h], g * GOT)
                    v.scalar_tensor_tensor(out=index[h][:, :], in0=i[:, 1, :], scalar=float(SLOTS),
                                           in1=i[:, 2, :], op0=ALU.mult, op1=ALU.add).then_inc(s_idx[h], 1)
            dve.wait_ge(s_starts, 1)
            link(v.tensor_copy(cnt[:, 3:4], bank[7][:, 0:1]))
            for n, at in enumerate(range(0, TILES, 512)):
                w = min(512, TILES - at)
                for q in range(0, w, PARTS):
                    m = min(PARTS, w - q)
                    last = v.tensor_scalar(started[:, q:q + m], iota_f[:, 0:m], float(at + q), cnt[:, 3:4],
                                           ALU.add, ALU.is_ge)
                last.then_inc(s_blk, 1)
                dve.wait_ge(s_blkuse, n + 1)
                link(v.tensor_copy(block_of[0:1, at:at + w], bank[5][0:1, 0:w]))
            v.memset(block_of[0:1, TILES:TILES + AHEAD], BLOCKS - 1)
            steps_wide = [1, TILES // U, U]
            by_step = block_of[0:1, 0:TILES].rearrange("p (t k) -> p t k", k=U)
            spots = spot_of[0:1, :].rearrange("p (t k) -> p t k", k=U)
            link(v.tensor_tensor(spots, by_step, by_step[:, :, 0:1].to_broadcast(steps_wide), ALU.subtract))
            link(v.tensor_scalar(spot_of[0:1, :], spot_of[0:1, :], float(HID), None, ALU.mult))
            dve.wait_ge(s_back, 16)
            slot_col = slots_in[:, 0:TILES, 1]
            v.tensor_copy(row_lo[:, 0:TILES], slots_in[:, 0:TILES, 0])
            v.memset(col_lo[:, TILES:COL_GROUPS * PARTS], 0.0)
            v.tensor_scalar(col_id[:, 0:TILES], slot_col, PARTS - 1, None, ALU.bitwise_and)
            link(v.tensor_scalar(col_tmp, slot_col, shift, None, ALU.logical_shift_right))
            v.tensor_copy(col_lo[:, 0:TILES], col_id[:, 0:TILES])
            link(v.tensor_copy(col_hi[:, 0:TILES], col_tmp))
            link(v.scalar_tensor_tensor(out=col_id[:, 0:TILES], in0=col_id[:, 0:TILES], scalar=float(NB),
                                        in1=col_tmp, op0=ALU.mult, op1=ALU.add))
            v.tensor_copy(x_cur[:, :, :], total[:, :, :]).then_inc(s_edges, 1)
            dve.wait_ge(s_edges, 1)
            dve.wait_ge(t_table, 16)

            k_blk, g_blk = dve.alloc_register("k_blk"), dve.alloc_register("g_blk")
            with dve.Fori(0, LAYERS) as l:
                for cur, every in ((w_cur, w_all), (a1_cur, a1_all), (b1_cur, b1_all), (a2_cur, a2_all)):
                    v.tensor_copy(cur[:, :], every[:, ds(l, 1), :].rearrange("p o d -> p (o d)"))
                v.tensor_copy(bias_cur[:, :], bias_all[:, ds(l, 1)])
                v.tensor_copy(b2_cur[:, :], b2_all[:, ds(l, 1)]).then_inc(n_cur, 1)
                dve.wait_ge(n_cur, l + 1)
                v.tensor_tensor(total[:, :, :], total[:, :, :], x_cur[:, :, :], ALU.add).then_inc(l_end, 1)
                with dve.Fori(0, NODE_STEPS) as b:
                    n = l * NODE_STEPS + b
                    for h in range(2):
                        e = Steps(n_ch, (n * 2 + h) * 5)
                        part = p3v[:, ds((b * 2 + h) * GRP, GRP), :, :]
                        both = bank[4 + h][:, :].rearrange("p (g d) -> p g d", g=GRP)
                        dve.wait_ge(n_pq[h], n + 1)
                        e.mark(v.tensor_tensor(rest[h][:, 0], both[:, :, 0:HID],
                                               b1_cur[:, :].unsqueeze(1).to_broadcast([PARTS, GRP, HID]), ALU.add))
                        dve.wait_ge(n_qst[h], n * 16)
                        v.tensor_copy(q_step[h][:, :, :], both[:, :, HID:2 * HID]).then_inc(n_q[h], 1)
                        e.wait(dve)
                        link(v.tensor_copy(part[:, :, 0, :], rest[h][:, 0]), e)
                        link(v.tensor_tensor(rest[h][:, 1], rest[h][:, 0], part[:, :, 0, :],
                                             ALU.subtract), e)
                        link(v.tensor_copy(part[:, :, 1, :], rest[h][:, 1]), e)
                        e.mark(v.tensor_tensor(part[:, :, 2, :], rest[h][:, 1], part[:, :, 1, :], ALU.subtract))
                def spread_onehot(h, at, freed):
                    dve.wait_ge(a_row[h], freed)
                    build_onehot(onehot[h], row_lo[:, ds(at, U)]).then_inc(a_onehot[h], 1)

                spread_onehot(0, 0, l * A_STEPS)
                v.memset(acc[:, :, :], 0.0).then_inc(l_end, 1)
                with dve.Fori(0, A_STEPS) as b:
                    g = l * A_STEPS + b
                    for h in range(2):
                        at = (b * 2 + h) * U
                        e = Steps(a_ch, (g * 2 + h) * 9)
                        sm, m3 = small[h], mask3[h]
                        spread_onehot(1 - h, (b * 2 + (h + 1)) * U, g + h)
                        dve.wait_ge(a_p[h], [l * (A_STEPS + 1) + b, g][h] + 1)
                        dve.wait_ge(a_got[h], (g + 1) * GOT)
                        v.tensor_tensor(hidden[h][:, :, :], bank_p[h], got[h][:, :, 0:HID], ALU.add).then_inc(a_add[h], 1)
                        dve.wait_ge(a_add[h], g + 1)
                        link(v.scalar_tensor_tensor(out=hidden[h][:, :, :], in0=hidden[h][:, :, :], scalar=0.0,
                                                    in1=a2_cur[:, :].unsqueeze(1).to_broadcast([PARTS, U, HID]),
                                                    op0=ALU.max, op1=ALU.mult), e)
                        link(v.tensor_reduce(sm[:, 0, :], hidden[h][:, :, :], AX.X, ALU.add), e)
                        v.tensor_scalar(sm[:, 7, :], sm[:, 0, :], b2_cur[:, :], -80.0, ALU.add,
                                        ALU.max).then_inc(a_sum[h], 1)
                        dve.wait_ge(a_sig[h], g + 1)
                        link(v.tensor_scalar(sm[:, 5, :], sm[:, 1, :], 1.0, None, ALU.add), e)
                        link(v.reciprocal(sm[:, 6, :], sm[:, 5, :]), e)
                        link(v.tensor_scalar(sm[:, 2, :], sm[:, 6, :], ZETA - GAMMA, GAMMA, ALU.mult, ALU.add), e)
                        link(v.tensor_scalar(sm[:, 3, :], sm[:, 2, :], 0.0, 1.0, ALU.max, ALU.min), e)
                        v.tensor_copy(mask[:, ds(at, U)], sm[:, 3, :])
                        link(v.tensor_copy(m3[:, :, 0], sm[:, 3, :]), e)
                        link(v.tensor_tensor(sm[:, 4, :], sm[:, 3, :], m3[:, :, 0], ALU.subtract), e)
                        link(v.tensor_copy(m3[:, :, 1], sm[:, 4, :]), e)
                        v.tensor_tensor(m3[:, :, 2], sm[:, 4, :], m3[:, :, 1], ALU.subtract).then_inc(a_m3[h], 1)
                e = Steps(m_ch, l * 7)
                dve.wait_ge(m_rows, l + 1)
                sums = bank_r[:, 0:4 * NB].rearrange("p (b s) -> p b s", s=4)
                link(v.tensor_reduce(rows_sum[:, :], sums[:, :, 0:3], AX.X, ALU.add), e)
                e.mark(v.tensor_scalar(rows_sum[:, :], rows_sum[:, :], 1e-6, None, ALU.add))
                dve.wait_ge(m_sqrt, l + 1)
                link(v.reciprocal(stat[:, 1, :], stat[:, 0, :]), e)
                link(v.tensor_scalar(d_node[:, :], stat[:, 1, :], 10.0, None, ALU.min), e)
                d_wide = d_node[:, :].unsqueeze(2).to_broadcast([PARTS, NB, HID])
                v.tensor_tensor(x_cur[:, :, :], x_cur[:, :, :], d_wide, ALU.mult).then_inc(m_y, 1)
                link(v.tensor_copy(d3[:, 0, :], d_node[:, :]), e)
                link(v.tensor_tensor(stat[:, 2, :], d_node[:, :], d3[:, 0, :], ALU.subtract), e)
                link(v.tensor_copy(d3[:, 1, :], stat[:, 2, :]), e)
                v.tensor_tensor(d3[:, 2, :], stat[:, 2, :], d3[:, 1, :], ALU.subtract).then_inc(m_d, 1)
                def look_onehot(b, i):
                    k = b * 6 + i
                    dve.wait_ge(*columns_in(l, b, i))
                    if not isinstance(k, int):
                        dve.wait_ge(k_rows, l * (2 * (K_STEPS + 2)) + (k - 1) * 2)
                    v.tensor_scalar(onehot_t[i % 2][:, :, :], k_cols[i % 3], part_f[:, :], None,
                                    ALU.is_equal).then_inc(turned(l, b, i)[0], 1)

                def look_up(j, k, at):
                    for q in range(2):
                        dve.wait_ge(k_rows, l * (2 * (K_STEPS + 2)) + k * 2 + (q + 1))
                        if q == 0 and not isinstance(k, int):
                            dve.wait_ge(k_sel, l * (2 * (K_STEPS + 1)) + k * 2)
                        for i in range(q * (U // 2), (q + 1) * (U // 2)):
                            last = v.scalar_tensor_tensor(
                                out=picked[:, i, :], in0=iota_b[:, 0:NB], scalar=col_hi[:, ds(at + i, 1)],
                                in1=bank_d[j][q][:, i % (U // 2), 0:NB], op0=ALU.is_equal, op1=ALU.mult,
                                accum_out=k_weight[j][:, 0, i:i + 1])
                        last.then_inc(k_sel, 1)

                def weigh(j, k, at):
                    dve.wait_ge(k_sel, l * (2 * (K_STEPS + 1)) + k * 2 + 2)
                    v.tensor_tensor(k_weight[j][:, 1, :], k_weight[j][:, 0, :], mask[:, ds(at, U)],
                                    ALU.mult).then_inc(k_wt, 1)

                def join(blk, sums):
                    first = dve.snap(blk, min_val=0, max_val=BLOCKS - 1)
                    some = acc[:, ds(first, U), :].rearrange("p b d -> p (b d)")
                    return v.tensor_tensor(some, some, sums[:, :], ALU.add)

                def join_last(b, i):
                    if i % 3 == 0:
                        dve.wait_ge(g_acc, l * QUADS + (b * 2 + i // 3))
                    dve.wait_ge(*joined(l, b, i - 2))
                    dve.wait_ge(*summed(l, b, i - 1))
                    join(k_blk, bank[1 + (i - 1) % 2]).then_inc(k_acc[(i - 1) % 2], 1)

                look_onehot(0, 0)
                look_up(0, 0, 0)
                weigh(0, 0, 0)
                build_onehot(k_hot[0], row_lo[:, 0:U]).then_inc(k_w, 1)
                dve.wait_ge(l_end, l * 3 + 2)
                dve.sem_inc(dve_go, 1)
                dve.load(k_blk, block_of[0:1, 0:1])
                with dve.Fori(0, B_BODIES) as b:
                    for i in range(6):
                        k = b * 6 + i
                        at, next_at = look_step(b, i) * U, look_step(b, i + 1) * U
                        if i % 3 == 1:
                            dve.wait_ge(g_o[1 - i // 3], l * B_BODIES + (b + i // 3))
                            at_g = (b * 8 + (4 * (i // 3) + 3)) * U
                            build_onehot(g_hot, row_lo[:, ds(at_g, U)]).then_inc(g_w, 1)
                            look_onehot(b, i + 2)
                        look_up((i + 1) % 2, k + 1, next_at)
                        build_onehot(k_hot[(i + 1) % 2], row_lo[:, ds(next_at, U)]).then_inc(k_w, 1)
                        join_last(b, i)
                        weigh((i + 1) % 2, k + 1, next_at)
                        dve.load(k_blk, block_of[0:1, ds(at, 1)])
                        if i % 3 == 2:
                            dve.load(g_blk, block_of[0:1, ds(at_g, 1)])
                            dve.wait_ge(*joined(l, b, i - 1))
                            dve.wait_ge(g_o[i // 3], l * B_BODIES + b + 1)
                            join(g_blk, bank[3]).then_inc(g_acc, 1)
                join_last(B_BODIES, 0)
                dve.wait_ge(*joined(l, B_BODIES, -1))
                dve.wait_ge(k_rows, (l + 1) * (2 * (K_STEPS + 2)))
                dve.wait_ge(m_yst, (l + 1) * 16)
                v.tensor_tensor(x_cur[:, :, :], acc[:, 0:NB, :], d_wide, ALU.mult).then_inc(l_end, 1)
                dve.wait_ge(l_end, l * 3 + 3)
            e = Steps(f_ch)
            wide = [PARTS, NB // PIECES, HID]
            for c in range(PIECES + 1):
                if c < PIECES:
                    some = piece(c)
                    mean = stat[:, 3, some].unsqueeze(2).to_broadcast(wide)
                    link(v.tensor_tensor(total[:, some, :], total[:, some, :], x_cur[:, some, :], ALU.add), e)
                    link(v.tensor_reduce(stat[:, 0, some], total[:, some, :], AX.X, ALU.add), e)
                    link(v.tensor_scalar(stat[:, 3, some], stat[:, 0, some], 1.0 / HID, None, ALU.mult), e)
                    v.tensor_tensor(total[:, some, :], total[:, some, :], mean, ALU.subtract).then_inc(f_mid, 1)
                if c > 0:
                    some = piece(c - 1)
                    scale = stat[:, 0, some].unsqueeze(2).to_broadcast(wide)
                    dve.wait_ge(f_sq, c)
                    v.tensor_reduce(stat[:, 1, some], acc[:, some, :], AX.X, ALU.add).then_inc(f_var, 1)
                    dve.wait_ge(f_sqrt, c)
                    link(v.reciprocal(stat[:, 0, some], stat[:, 2, some]), e)
                    v.tensor_tensor(total[:, some, :], total[:, some, :], scale, ALU.mult).then_inc(f_out, 1)


NAMES = {"x": "x", "src": "src", "dst": "dst", "L0_gnn_nb_W": "nb_W", "L0_gnn_nb_b": "nb_b",
         "L0_gnn_self_W": "self_W", "L0_gnn_self_b": "self_b", "L0_gnn_att1_W": "att1_W",
         "L0_gnn_att1_b": "att1_b", "L0_gnn_att2_W": "att2_W", "L0_gnn_att2_b": "att2_b"}


def kernel(**inputs):
    import numpy as np
    import concourse.bacc as bacc
    from concourse.bass_utils import run_bass_kernel_spmd

    nc = bacc.Bacc("TRN2", target_bir_lowering=False, num_devices=1)
    arrays, args = {}, {}
    for name, arg in NAMES.items():
        a = np.ascontiguousarray(inputs[name])
        arrays[f"in_{arg}"] = a
        args[arg] = nc.dram_tensor(f"in_{arg}", a.shape, mybir.dt.from_np(a.dtype), kind="ExternalInput").ap()
    shape = inputs["x"].shape
    args["out"] = nc.dram_tensor("out_0", shape, F32, kind="ExternalOutput").ap()
    build(nc, **args)
    r = run_bass_kernel_spmd(nc, [arrays], core_ids=[0])
    return r.results[0]["out_0"]
```
